# Optimizing a Trainium2 kernel written in Bass

```python
import numpy as np
import jax
import jax.numpy as jnp

def _softmax(x, axis=-1):
    return jax.nn.softmax(x, axis=axis)

def _gelu(x):
    return jax.nn.gelu(x, approximate=True)

def _silu(x):
    return jax.nn.silu(x)

def _sigmoid(x):
    return jax.nn.sigmoid(x)

def _layernorm(x, axis=-1, eps=1e-05):
    m = jnp.mean(x, axis=axis, keepdims=True)
    v = jnp.var(x, axis=axis, keepdims=True)
    return (x - m) / jnp.sqrt(v + eps)

def _scatter_add(tgt, idx, src, axis=0):
    return tgt.at[idx].add(src)

def _segment_sum(src, seg, n):
    return jax.ops.segment_sum(src, seg, n)
kernel_name = 'mk_sandwich_d1_jaxref_r8_9905da'

def setup_inputs(seed: int=0):
    np.random.seed(seed)
    _w = jnp.asarray

    def _L0_attn_setup():
        import jax, jax.numpy as jnp
        import numpy as np
        B, N, D = (8, 256, 128)
        key = jax.random.key(seed)
        k1, k2, k3, k4 = jax.random.split(key, 4)
        data = jax.random.normal(k1, (B, N, D), dtype=jnp.float32)
        W1 = jax.random.normal(k2, (1, D), dtype=jnp.float32) * 0.02
        b1 = jnp.zeros((D,), dtype=jnp.float32)
        W2 = jax.random.normal(k3, (2 * D, D), dtype=jnp.float32) * 0.02
        return {'data': data, 'W1': W1, 'b1': b1, 'W2': W2}
    _L0_attn_in = _L0_attn_setup()

    def _L0_ffn_setup():
        import jax, jax.numpy as jnp
        import numpy as np
        D_IN, D_HID = (128, 512)

        def _ternary(key, shape):
            return jax.random.randint(key, shape, -1, 2).astype(jnp.float32)

        def _tlin(x, w, s):
            return jnp.einsum('bsi,oi->bso', x, w) * s
        key = jax.random.key(seed)
        ks = jax.random.split(key, 12)
        inv = lambda fan: 1.0 / np.sqrt(fan).astype(np.float32)
        return {'x': jax.random.normal(ks[0], (4, 256, D_IN), dtype=jnp.float32), 'w1_w': _ternary(ks[1], (D_HID, D_IN)), 'w1_s': jax.random.uniform(ks[2], (D_HID,), dtype=jnp.float32) * inv(D_IN), 'w2_w': _ternary(ks[3], (D_HID, D_IN)), 'w2_s': jax.random.uniform(ks[4], (D_HID,), dtype=jnp.float32) * inv(D_IN), 'h1_w': _ternary(ks[5], (D_HID, D_HID)), 'h1_s': jax.random.uniform(ks[6], (D_HID,), dtype=jnp.float32) * inv(D_HID), 'h2_w': _ternary(ks[7], (D_HID, D_HID)), 'h2_s': jax.random.uniform(ks[8], (D_HID,), dtype=jnp.float32) * inv(D_HID), 'w3_w': _ternary(ks[9], (D_IN, D_HID)), 'w3_s': jax.random.uniform(ks[10], (D_IN,), dtype=jnp.float32) * inv(D_HID)}
    _L0_ffn_in = _L0_ffn_setup()
    _d = {'L0_attn_data': _L0_attn_in['data'], 'L0_attn_W1': _L0_attn_in['W1'], 'L0_attn_b1': _L0_attn_in['b1'], 'L0_attn_W2': _L0_attn_in['W2'], 'L0_ffn_w1_w': _L0_ffn_in['w1_w'], 'L0_ffn_w1_s': _L0_ffn_in['w1_s'], 'L0_ffn_w2_w': _L0_ffn_in['w2_w'], 'L0_ffn_w2_s': _L0_ffn_in['w2_s'], 'L0_ffn_h1_w': _L0_ffn_in['h1_w'], 'L0_ffn_h1_s': _L0_ffn_in['h1_s'], 'L0_ffn_h2_w': _L0_ffn_in['h2_w'], 'L0_ffn_h2_s': _L0_ffn_in['h2_s'], 'L0_ffn_w3_w': _L0_ffn_in['w3_w'], 'L0_ffn_w3_s': _L0_ffn_in['w3_s']}
    _x0 = _d['L0_attn_data']
    _d['L0_attn_data'] = jax.random.normal(jax.random.fold_in(jax.random.key(seed), 1), (2, 1024, 128), dtype=_x0.dtype)
    del _x0
    return _d

def reference(L0_attn_data, L0_attn_W1, L0_attn_b1, L0_attn_W2, L0_ffn_w1_w, L0_ffn_w1_s, L0_ffn_w2_w, L0_ffn_w2_s, L0_ffn_h1_w, L0_ffn_h1_s, L0_ffn_h2_w, L0_ffn_h2_s, L0_ffn_w3_w, L0_ffn_w3_s):

    def _L0_attn_ref(data, W1, b1, W2):
        import jax, jax.numpy as jnp
        import numpy as np
        B, N, D = (8, 256, 128)
        sq = jnp.sum(data * data, axis=-1, keepdims=True)
        normed = data * jax.lax.rsqrt(jnp.maximum(sq, 1e-12))
        sim = jnp.einsum('bnd,bmd->bnm', normed, normed)
        counter = jnp.sum(jax.nn.relu(sim), axis=-1, keepdims=True)
        counter = jax.nn.softplus(counter @ W1 + b1)
        out = jnp.concatenate([data, counter], axis=-1) @ W2
        return out

    def _L0_ffn_ref(x, w1_w, w1_s, w2_w, w2_s, h1_w, h1_s, h2_w, h2_s, w3_w, w3_s):
        import jax, jax.numpy as jnp
        import numpy as np
        D_IN, D_HID = (128, 512)

        def _ternary(key, shape):
            return jax.random.randint(key, shape, -1, 2).astype(jnp.float32)

        def _tlin(x, w, s):
            return jnp.einsum('bsi,oi->bso', x, w) * s
        h = jax.nn.silu(_tlin(x, w1_w, w1_s)) * _tlin(x, w2_w, w2_s)
        h = jax.nn.gelu(_tlin(h, h1_w, h1_s), approximate=False)
        h = jax.nn.gelu(_tlin(h, h2_w, h2_s), approximate=False)
        return _tlin(h, w3_w, w3_s)
    x = L0_attn_data
    x = x + _layernorm(_L0_attn_ref(_layernorm(x, axis=-1), L0_attn_W1, L0_attn_b1, L0_attn_W2), axis=-1)
    x = x + _layernorm(_L0_ffn_ref(_layernorm(x, axis=-1), L0_ffn_w1_w, L0_ffn_w1_s, L0_ffn_w2_w, L0_ffn_w2_s, L0_ffn_h1_w, L0_ffn_h1_s, L0_ffn_h2_w, L0_ffn_h2_s, L0_ffn_w3_w, L0_ffn_w3_s), axis=-1)
    return x

_drawn_inputs = setup_inputs


def setup_inputs(seed=0):
    import zlib

    import numpy as np

    out = dict(_drawn_inputs(seed))
    spreads = {'L0_attn_b1': (0.0, 0.269)}
    factors = {}
    for name, (base, spread) in spreads.items():
        noise = np.random.default_rng([zlib.crc32(name.encode()), seed]).standard_normal(out[name].shape)
        drawn = base * np.exp(spread * noise) if base else spread * noise
        out[name] = jnp.asarray(drawn.astype(out[name].dtype))
    for name, factor in factors.items():
        out[name] = (out[name] * factor).astype(out[name].dtype)
    return out
```

```python
from contextlib import ExitStack

import concourse.bass as bass
from concourse import mybir

ALU = mybir.AluOpType
ACT = mybir.ActivationFunctionType
AX = mybir.AxisListType
F32 = mybir.dt.float32
F16 = mybir.dt.float16
I32 = mybir.dt.int32

P = 128
EPS = 1e-5
MIN_SQ = 1e-12
N_SCALE = 256.0
W_SCALE = 64.0
LO_SCALE = 2048.0
GT = 4
GW = GT * P


def build(nc, data, identity, cols, attn_w, up_w, h1_w, h2_w, w3_w, s3_row, out):
    D = data.shape[1]
    HID = w3_w.shape[0]
    assert D == P
    M = HID // P
    G = data.shape[0] // GW
    BG = 2
    B = G // BG
    BT = BG * GT
    BW = BG * GW

    units = []
    for i in range(BT):
        for half in range(2):
            first = i * P + half * GW
            if first < BW:
                units.append((i, half, first, min(GW, BW - first)))
    NU = len(units)
    NA = NU - 1

    NS = 2 * HID // 512 + 2 * M + M * D // 512

    x_dram = data.rearrange("(g p t) d -> g p t d", p=P, t=GT)
    out_dram = out.rearrange("(g p t) d -> g p t d", p=P, t=GT)

    with ExitStack() as ctx:
        def sb(name, shape, dt=F32):
            return ctx.enter_context(nc.sbuf_tensor(name, shape, dt))

        def sem(name):
            return ctx.enter_context(nc.semaphore(name))

        x = sb("x", [P, G, GT, D])
        x1 = sb("x1", [P, G, GT, D])
        ident = sb("ident", [P, P])
        ones = sb("ones", [P, P])
        neg_half = sb("neg_half", [P, 2 * GT])
        col = sb("col", [P, 4 * M + 2])
        colk = sb("colk", [P, 4 * M + 1])
        s3b = sb("s3b", [P, D])
        wf = sb("wf", [P, NS * 512])
        w_hi = sb("w_hi", [P, NS * 512], F16)
        w_his = sb("w_his", [P, NS * 512], F16)
        w_lo = sb("w_lo", [P, NS * 512], F16)
        w64 = sb("w64", [P, 2, 512])
        lo_sq = sb("lo_sq", [P, NS])
        lo_any = sb("lo_any", [P, 2])
        flag = sb("flag", [1, 1])
        aw = sb("aw", [P, 2 * D])
        aw_hi = sb("aw_hi", [P, 2 * D], F16)
        aw_lo = sb("aw_lo", [P, 2 * D], F16)
        stats = sb("stats", [P, 4, 2, GT, 6])
        mv = sb("mv", [P, 4, G, GT, 2])
        base0 = sb("base0", [P, G, 2 * GT])
        small = sb("small", [P, G, GT])
        pow0 = sb("pow0", [P, G, 2 * GT])
        gq = sb("gq", [P, G, GT])
        base = sb("base", [P, 3, G, GT])
        rstd = sb("rstd", [P, 3, G, GT])
        nrm = sb("nrm", [P, 2, GT, D])
        n_hi = sb("n_hi", [P, G * GW], F16)
        n_lo = sb("n_lo", [P, G * GW], F16)
        junk = sb("junk", [P, 2, 512], F16)
        relu = sb("relu", [P, 4, 512])
        rows = sb("rows", [P, B, 2, BT])
        row = sb("row", [P, B, BT])
        acc = sb("acc", [P, B, BW])
        z_abs = sb("z_abs", [P, 2, GW])
        z_pos = sb("z_pos", [P, 2, GW])
        sp = sb("sp", [P, 2, GW])
        sp_hi = sb("sp_hi", [P, 2, GW], F16)
        sp_lo = sb("sp_lo", [P, 2, GW], F16)
        y = sb("y", [P, 2, GT, D])
        y2 = sb("y2", [P, 2, GT, D])
        a_hi = sb("a_hi", [P, G, GW], F16)
        a_lo = sb("a_lo", [P, G, GW], F16)
        act_f = sb("act_f", [P, 4, GW])
        gate_f = sb("gate_f", [P, 2, GW])
        ho_hi = sb("ho_hi", [P, BG, M, GW], F16)
        ho_lo = sb("ho_lo", [P, BG, M, GW], F16)
        he_hi = sb("he_hi", [P, BG, M, GW], F16)
        he_lo = sb("he_lo", [P, BG, M, GW], F16)
        sink = sb("sink", [P, 2 * G * M + G])

        ps_sim = ctx.enter_context(nc.psum_tensor("ps_sim", [P, 2, 512], F32))
        ps_tr = ctx.enter_context(nc.psum_tensor("ps_tr", [P, 512], F32))
        ps_at = ctx.enter_context(nc.psum_tensor("ps_at", [P, 512], F32))
        ps_ff = ctx.enter_context(nc.psum_tensor("ps_ff", [P, 4, 512], F32))

        x_in = [sem(f"x_in{g}") for g in range(G)]
        ident_in, cols_in, aw_in, s3_in, up_in, h1_in, h2_in, w3_in = (
            sem(n) for n in ("ident_in", "cols_in", "aw_in", "s3_in", "up_in", "h1_in", "h2_in", "w3_in"))
        consts_set = sem("consts_set")
        rows_zeroed = sem("rows_zeroed")
        base_ready = [sem(f"base_ready{n}") for n in range(4)]
        pow_ready = [sem(f"pow_ready{n}") for n in range(4)]
        gq_step = sem("gq_step")
        gq_ready = sem("gq_ready")
        nrm_ready = sem("nrm_ready")
        nT_ready = sem("nT_ready")
        n_hi_ready = sem("n_hi_ready")
        n_lo_ready = sem("n_lo_ready")
        sim_ready = sem("sim_ready")
        relu_done = sem("relu_done")
        acc_done = sem("acc_done")
        diag_done = sem("diag_done")
        count_ready = sem("count_ready")
        z_read = sem("z_read")
        softplus_step = sem("softplus_step")
        softplus_log = sem("softplus_log")
        sp_ready = sem("sp_ready")
        sp_hi_ready = sem("sp_hi_ready")
        sp_lo_ready = sem("sp_lo_ready")
        pa_ready = sem("pa_ready")
        pb_ready = sem("pb_ready")
        y_done = sem("y_done")
        y2_done = sem("y2_done")
        a_rows_ready = sem("a_rows_ready")
        aT_ready = sem("aT_ready")
        a_hi_ready = sem("a_hi_ready")
        a_lo_ready = sem("a_lo_ready")
        aw_hi_ready = sem("aw_hi_ready")
        aw_lo_ready = sem("aw_lo_ready")
        w_hi_ready = sem("w_hi_ready")
        w_lo_step = sem("w_lo_step")
        w_lo_ready = sem("w_lo_ready")
        lo_sq_ready = sem("lo_sq_ready")
        lo_any_ready = sem("lo_any_ready")
        lo_all_ready = sem("lo_all_ready")
        flag_ready = sem("flag_ready")
        colk_ready = sem("colk_ready")
        up_ready = sem("up_ready")
        silu_done = sem("silu_done")
        gate_done = sem("gate_done")
        up_hi_ready = sem("up_hi_ready")
        up_lo_ready = sem("up_lo_ready")
        hid_ready = sem("hid_ready")
        gelu_done = sem("gelu_done")
        hid_hi_ready = sem("hid_hi_ready")
        hid_lo_ready = sem("hid_lo_ready")
        down_ready = sem("down_ready")
        down_read = sem("down_read")
        out_ready = sem("out_ready")
        out_stored = sem("out_stored")
        vec_step = sem("vec_step")

        N_UP, N_HID = 2 * HID // 512, M
        off_up = 0
        off_hid = [N_UP * 512, (N_UP + N_HID) * 512]
        off_w3 = (N_UP + 2 * N_HID) * 512
        slice_in = [up_in] * N_UP + [h1_in] * N_HID + [h2_in] * N_HID + [w3_in]

        def hid_index(layer, g, m):
            b, i = divmod(g, BG)
            return ((b * 2 + layer) * BG + i) * M + m

        def acc_count(n):
            b, u = divmod(n, NU)
            return b * NA + min(u + 1, NA)

        block = ctx.enter_context(nc.Block())

        @block.sync
        def _(sp_):
            for g in range(G):
                sp_.dma_start(x[:, g], x_dram[g]).then_inc(x_in[g], 16)
                if g == 0:
                    sp_.dma_start(ident[:], identity).then_inc(ident_in, 16)
                if g == 1:
                    sp_.dma_start(col[:], cols).then_inc(cols_in, 16)
                    sp_.dma_start(aw[:].rearrange("p (k n) -> p k n", k=2), attn_w).then_inc(aw_in, 16)
            sp_.dma_start(wf[:, 0:N_UP * 512], up_w).then_inc(up_in, 16)
            for off, w, s in ((off_hid[0], h1_w, h1_in), (off_hid[1], h2_w, h2_in)):
                sp_.dma_start(wf[:, off:off + M * HID].rearrange("p (k n) -> p k n", k=M),
                              w.rearrange("(k p) n -> p k n", p=P)).then_inc(s, 16)
            sp_.dma_start(wf[:, off_w3:off_w3 + M * D].rearrange("p (k n) -> p k n", k=M),
                          w3_w.rearrange("(k p) n -> p k n", p=P)).then_inc(w3_in, 16)
            sp_.dma_start(s3b[:], s3_row.partition_broadcast(P)).then_inc(s3_in, 16)
            for g in range(G):
                sp_.wait_ge(out_ready, g + 1)
                sp_.dma_start(out_dram[g], x1[:, g]).then_inc(out_stored, 16)
            sp_.wait_ge(out_stored, 16 * G)

        @block.gpsimd
        def _(pool):
            def power(n, g):
                pool.wait_ge(base_ready[n], g + 1)
                if n == 0:
                    nc.gpsimd.tensor_tensor(pow0[:, g], base0[:, g], neg_half[:], ALU.pow).then_inc(pow_ready[0], 1)
                    pool.wait_ge(pow_ready[0], g + 1)
                    nc.gpsimd.tensor_tensor(gq[:, g], pow0[:, g, 0:GT], pow0[:, g, GT:2 * GT],
                                            ALU.mult).then_inc(gq_step, 1)
                    pool.wait_ge(gq_step, g + 1)
                    nc.gpsimd.tensor_tensor(gq[:, g], gq[:, g], base0[:, g, 0:GT], ALU.mult).then_inc(gq_ready, 1)
                else:
                    nc.gpsimd.tensor_tensor(rstd[:, n - 1, g], base[:, n - 1, g], neg_half[:, 0:GT],
                                            ALU.pow).then_inc(pow_ready[n], 1)

            def weight_lo(s):
                pool.wait_ge(slice_in[s], 16)
                if s >= 2:
                    pool.wait_ge(w_lo_ready, s - 1)
                nc.gpsimd.tensor_scalar(w64[:, s % 2], wf[:, 512 * s:512 * s + 512], W_SCALE, 0.0,
                                        ALU.mult, ALU.add).then_inc(w_lo_step, 1)
                pool.wait_ge(w_lo_step, s + 1)
                pool.wait_ge(w_hi_ready, s + 1)
                nc.gpsimd.tensor_tensor(w_lo[:, 512 * s:512 * s + 512], w64[:, s % 2],
                                        w_hi[:, 512 * s:512 * s + 512], ALU.subtract).then_inc(w_lo_ready, 1)

            def softplus_hi(g):
                pool.wait_ge(sp_ready, g + 1)
                nc.gpsimd.tensor_scalar(sp_hi[:, g % 2], sp[:, g % 2], 1.0, 0.0,
                                        ALU.mult, ALU.add).then_inc(sp_hi_ready, 1)

            def up_hi(g):
                for m in range(M):
                    n = M * g + m
                    pool.wait_ge(gate_done, n + 1)
                    nc.gpsimd.tensor_scalar(ho_hi[:, g % BG, m], gate_f[:, n % 2], 1.0 / LO_SCALE, 0.0,
                                            ALU.mult, ALU.add).then_inc(up_hi_ready, 1)

            def hid_hi(layer, g):
                dst = (he_hi, ho_hi)[layer]
                for m in range(M):
                    n = hid_index(layer, g, m)
                    pool.wait_ge(gelu_done, n + 1)
                    nc.gpsimd.tensor_scalar(dst[:, g % BG, m], act_f[:, n % 4], 1.0, 0.0,
                                            ALU.mult, ALU.add).then_inc(hid_hi_ready, 1)

            nc.gpsimd.memset(neg_half[:], -0.5).then_inc(consts_set, 1)
            nc.gpsimd.memset(ones[:], 1.0).then_inc(consts_set, 1)
            nc.gpsimd.memset(rows[:], 0.0).then_inc(rows_zeroed, 1)
            pool.wait_ge(consts_set, 1)
            power(0, 0)
            power(0, 1)
            for s in range(N_UP):
                weight_lo(s)
            power(0, 2)
            power(0, 3)
            for s in range(N_UP, NS):
                weight_lo(s)
            softplus_hi(0)
            softplus_hi(1)
            for g in (0, 1):
                power(1, g)
                power(2, g)
            up_hi(0)
            up_hi(1)
            hid_hi(0, 0)
            softplus_hi(2)
            softplus_hi(3)
            hid_hi(0, 1)
            power(1, 2)
            power(2, 2)
            hid_hi(1, 0)
            power(1, 3)
            power(2, 3)
            hid_hi(1, 1)
            power(3, 0)
            up_hi(2)
            power(3, 1)
            up_hi(3)
            for layer in (0, 1):
                for g in (2, 3):
                    hid_hi(layer, g)
            power(3, 2)
            power(3, 3)

        @block.scalar
        def _(act):

            def weight_hi(s):
                act.wait_ge(slice_in[s], 16)
                nc.scalar.activation(w_hi[:, 512 * s:512 * s + 512], wf[:, 512 * s:512 * s + 512], ACT.Copy,
                                     scale=W_SCALE).then_inc(w_hi_ready, 1)

            def weight_square(s):
                act.wait_ge(w_lo_ready, s + 1)
                if s >= 2:
                    act.wait_ge(lo_sq_ready, s - 1)
                nc.scalar.activation(junk[:, s % 2], w_lo[:, 512 * s:512 * s + 512], ACT.Square,
                                     accum_out=lo_sq[:, s:s + 1]).then_inc(lo_sq_ready, 1)

            def n_high(g):
                act.wait_ge(nT_ready, g + 1)
                nc.scalar.copy(n_hi[:, g * GW:(g + 1) * GW], (ps_tr, ps_at, ps_tr, ps_tr)[g][:]).then_inc(n_hi_ready, 1)

            def relu_sums(b, us):
                for u in us:
                    i, half, _, w = units[u]
                    n = b * NU + u
                    act.wait_ge(sim_ready, n + 1)
                    if n >= 4:
                        act.wait_ge(acc_done, acc_count(n - 4))
                        act.wait_ge(relu_done, n - 3)
                    else:
                        act.wait_ge(rows_zeroed, 1)
                    nc.scalar.activation(relu[:, n % 4, 0:w], ps_sim[:, n % 2, 0:w], ACT.Relu,
                                         accum_out=rows[:, b, half, i:i + 1]).then_inc(relu_done, 1)

            def softplus(g):
                act.wait_ge(count_ready, g + 1)
                act.wait_ge(colk_ready, 1)
                if g >= 2:
                    act.wait_ge(sp_ready, g - 1)
                w1c, b1c = colk[:, 4 * M:4 * M + 1], col[:, 4 * M + 1:4 * M + 2]
                nc.scalar.activation(z_abs[:, g % 2], ps_tr[:], ACT.Abs, bias=b1c,
                                     scale=w1c).then_inc(softplus_step, 1)
                nc.scalar.activation(z_pos[:, g % 2], ps_tr[:], ACT.Relu, bias=b1c, scale=w1c).then_inc(z_read, 1)
                act.wait_ge(softplus_step, 2 * g + 1)
                nc.scalar.activation(z_abs[:, g % 2], z_abs[:, g % 2], ACT.Exp, scale=-1.0).then_inc(softplus_step, 1)
                act.wait_ge(softplus_step, 2 * g + 2)
                nc.scalar.activation(z_abs[:, g % 2], z_abs[:, g % 2], ACT.Ln, bias=1.0).then_inc(softplus_log, 1)

            def a_high(g):
                act.wait_ge(aT_ready, g + 1)
                nc.scalar.copy(a_hi[:, g], ps_tr[:]).then_inc(a_hi_ready, 1)

            def silu(g):
                for m in range(M):
                    n = M * g + m
                    act.wait_ge(up_ready, 2 * n + 1)
                    if g == 2 and m < 4:
                        act.wait_ge(hid_lo_ready, hid_index(1, 1, m) + 1)
                        act.wait_ge(hid_hi_ready, hid_index(1, 1, m) + 1)
                    elif n >= 4:
                        act.wait_ge(gate_done, n - 3)
                    nc.scalar.activation(act_f[:, n % 4], ps_ff[:, 2 * (m % 2)], ACT.Silu,
                                         scale=colk[:, m:m + 1]).then_inc(silu_done, 1)

            def gelu(layer, g):
                for m in range(M):
                    n = hid_index(layer, g, m)
                    act.wait_ge(hid_ready, n + 1)
                    if layer == 0 and g % BG == 0:
                        act.wait_ge(gate_done, M * (g + 1) + m + 1)
                    else:
                        act.wait_ge(hid_lo_ready, n - 3)
                        act.wait_ge(hid_hi_ready, n - 3)
                    nc.scalar.activation(act_f[:, n % 4], ps_ff[:, m], ACT.Gelu,
                                         scale=colk[:, (2 + layer) * M + m:(2 + layer) * M + m + 1]
                                         ).then_inc(gelu_done, 1)

            act.wait_ge(aw_in, 16)
            nc.scalar.activation(aw_hi[:], aw[:], ACT.Copy, scale=W_SCALE).then_inc(aw_hi_ready, 1)
            n_high(0)
            n_high(1)
            for s in range(N_UP):
                weight_hi(s)
            relu_sums(0, range(0, NU // 2))
            for s in range(N_UP, N_UP + N_HID):
                weight_hi(s)
            relu_sums(0, range(NU // 2, NU))
            for s in range(N_UP + N_HID, NS):
                weight_hi(s)
            for s in range(N_UP):
                weight_square(s)
            softplus(0)
            softplus(1)
            for s in range(N_UP, NS):
                weight_square(s)
            a_high(0)
            a_high(1)
            n_high(2)
            n_high(3)
            silu(0)
            relu_sums(1, range(0, NU // 2))
            silu(1)
            relu_sums(1, range(NU // 2, NU))
            gelu(0, 0)
            softplus(2)
            softplus(3)
            gelu(0, 1)
            gelu(1, 0)
            a_high(2)
            gelu(1, 1)
            a_high(3)
            silu(2)
            silu(3)
            for layer in (0, 1):
                for g in (2, 3):
                    gelu(layer, g)

        @block.tensor
        def _(pe):
            def n_transpose(g):
                pe.wait_ge(nrm_ready, g + 1)
                if g == 0:
                    pe.wait_ge(ident_in, 16)
                if g == 2:
                    pe.wait_ge(a_lo_ready, 2)
                if g == 3:
                    pe.wait_ge(n_lo_ready, 3)
                dst = (ps_tr, ps_at, ps_tr, ps_tr)[g]
                for t in range(GT):
                    mm = nc.tensor.transpose(dst[:, t * P:(t + 1) * P], nrm[:, g % 2, t], ident[:])
                mm.then_inc(nT_ready, 1)

            def similarity(b, us):
                pe.wait_ge(n_lo_ready, BG * (b + 1))
                for u in us:
                    i, _, first, w = units[u]
                    n = b * NU + u
                    if n >= 2:
                        pe.wait_ge(relu_done, n - 1)
                    r = b * BW + i * P
                    c = b * BW + first
                    dst = ps_sim[:, n % 2, 0:w]
                    nc.tensor.matmul(dst, n_hi[:, r:r + P], n_hi[:, c:c + w], start=True, stop=False)
                    nc.tensor.matmul(dst, n_hi[:, r:r + P], n_lo[:, c:c + w], start=False, stop=False)
                    nc.tensor.matmul(dst, n_lo[:, r:r + P], n_hi[:, c:c + w], start=False,
                                     stop=True).then_inc(sim_ready, 1)

            def counter(g):
                pe.wait_ge(diag_done, GT * (g + 1))
                if g == 0:
                    pe.wait_ge(consts_set, 2)
                if g % 2 == 0:
                    pe.wait_ge(n_lo_ready, 1 if g == 0 else 4)
                else:
                    pe.wait_ge(z_read, g)
                b, i = divmod(g, BG)
                nc.tensor.matmul(ps_tr[:], ones[:], acc[:, b, i * GW:(i + 1) * GW], start=True,
                                 stop=True).then_inc(count_ready, 1)

            def row_product(dst, hi, lo, w):
                for t in range(GT):
                    o = dst[:, t * P:(t + 1) * P]
                    c = slice(t * P, (t + 1) * P)
                    nc.tensor.matmul(o, hi[:, c], aw_hi[:, w], start=True, stop=False)
                    nc.tensor.matmul(o, hi[:, c], aw_lo[:, w], start=False, stop=False)
                    mm = nc.tensor.matmul(o, lo[:, c], aw_hi[:, w], start=False, stop=True)
                return mm

            def attn_data(g):
                pe.wait_ge(aw_lo_ready, 1)
                if g == 0:
                    pe.wait_ge(n_lo_ready, 2)
                else:
                    pe.wait_ge(y2_done, g)
                c = slice(g * GW, (g + 1) * GW)
                row_product(ps_at, n_hi[:, c], n_lo[:, c], slice(0, D)).then_inc(pa_ready, 1)

            def attn_counter(g):
                pe.wait_ge(sp_hi_ready, g + 1)
                pe.wait_ge(sp_lo_ready, g + 1)
                pe.wait_ge(y_done, g + 1)
                row_product(ps_at, sp_hi[:, g % 2], sp_lo[:, g % 2], slice(D, 2 * D)).then_inc(pb_ready, 1)

            def a_transpose(g):
                pe.wait_ge(a_rows_ready, g + 1)
                if g % 2 == 0:
                    pe.wait_ge(z_read, g + 2)
                else:
                    pe.wait_ge(a_lo_ready, g)
                for t in range(GT):
                    mm = nc.tensor.transpose(ps_tr[:, t * P:(t + 1) * P], nrm[:, g % 2, t], ident[:])
                mm.then_inc(aT_ready, 1)

            def tail(general):
                def product(dst, w_col, hi, lo, first, last):
                    w = slice(w_col, w_col + P)
                    nc.tensor.matmul(dst, w_hi[:, w], hi, start=first, stop=False)
                    if general:
                        nc.tensor.matmul(dst, w_lo[:, w], hi, start=False, stop=False)
                    return nc.tensor.matmul(dst, w_his[:, w], lo, start=False, stop=last)

                def up(g):
                    pe.wait_ge(a_hi_ready, g + 1)
                    pe.wait_ge(a_lo_ready, g + 1)
                    for m in range(M):
                        n = M * g + m
                        if g == 2 and m == 0:
                            pe.wait_ge(down_read, 1)
                            pe.wait_ge(gelu_done, hid_index(1, 1, 1) + 1)
                        elif g == 2 and m == 1:
                            pe.wait_ge(gelu_done, hid_index(1, 1, 3) + 1)
                        elif n >= 2:
                            pe.wait_ge(gate_done, n - 1)
                        if g == 3 and m == 0:
                            pe.wait_ge(down_read, 2)
                        for j in range(2):
                            product(ps_ff[:, 2 * (m % 2) + j], off_up + j * HID + m * P, a_hi[:, g], a_lo[:, g],
                                    True, True).then_inc(up_ready, 1)

                def hidden(layer, g):
                    src_hi, src_lo = ((ho_hi, ho_lo), (he_hi, he_lo))[layer]
                    for m in range(M):
                        n = hid_index(layer, g, m)
                        if layer == 0 and g % BG == 0:
                            pe.wait_ge(gate_done, M * (g + 1) + 2 + m // 2 + 1)
                        else:
                            pe.wait_ge(gelu_done, n - M + 1)
                        for k in range(M):
                            if m == 0:
                                if layer == 0:
                                    pe.wait_ge(up_hi_ready, M * g + k + 1)
                                    pe.wait_ge(up_lo_ready, M * g + k + 1)
                                else:
                                    pe.wait_ge(hid_hi_ready, hid_index(0, g, k) + 1)
                                    pe.wait_ge(hid_lo_ready, hid_index(0, g, k) + 1)
                            mm = product(ps_ff[:, m], off_hid[layer] + k * HID + m * P, src_hi[:, g % BG, k],
                                         src_lo[:, g % BG, k], k == 0, k == M - 1)
                        mm.then_inc(hid_ready, 1)

                def down(g):
                    if g == 1:
                        pe.wait_ge(gate_done, M * 2 + 3)
                    elif g == 3:
                        pe.wait_ge(gelu_done, hid_index(1, 3, 1) + 1)
                    else:
                        pe.wait_ge(gelu_done, hid_index(1, g + 1, 0) + 1)
                    for k in range(M):
                        pe.wait_ge(hid_hi_ready, hid_index(1, g, k) + 1)
                        pe.wait_ge(hid_lo_ready, hid_index(1, g, k) + 1)
                    for t in range(GT):
                        o = ps_ff[:, g % 2, t * P:(t + 1) * P]
                        c = slice(t * P, (t + 1) * P)
                        for k in range(M):
                            w = slice(off_w3 + k * D, off_w3 + (k + 1) * D)
                            nc.tensor.matmul(o, ho_hi[:, g % BG, k, c], w_hi[:, w], start=(k == 0), stop=False)
                            if general:
                                nc.tensor.matmul(o, ho_hi[:, g % BG, k, c], w_lo[:, w], start=False, stop=False)
                            mm = nc.tensor.matmul(o, ho_lo[:, g % BG, k, c], w_his[:, w], start=False,
                                                  stop=(k == M - 1))
                    mm.then_inc(down_ready, 1)

                up(0)
                similarity(1, range(0, NU // 2))
                up(1)
                similarity(1, range(NU // 2, NU))
                hidden(0, 0)
                attn_data(2)
                counter(2)
                counter(3)
                hidden(0, 1)
                attn_counter(2)
                attn_data(3)
                hidden(1, 0)
                a_transpose(2)
                attn_counter(3)
                hidden(1, 1)
                a_transpose(3)
                down(0)
                up(2)
                down(1)
                up(3)
                for layer in (0, 1):
                    for g in (2, 3):
                        hidden(layer, g)
                down(2)
                down(3)

            n_transpose(0)
            n_transpose(1)
            attn_data(0)
            similarity(0, range(NU))
            counter(0)
            counter(1)
            attn_counter(0)
            a_transpose(0)
            attn_data(1)
            attn_counter(1)
            a_transpose(1)
            n_transpose(2)
            n_transpose(3)
            pe.wait_ge(lo_any_ready, 1)
            nc.tensor.matmul(ps_at[0:1, 0:2], lo_any[:, 0:1], ones[:, 0:2], start=True,
                             stop=True).then_inc(lo_all_ready, 1)
            pe.wait_ge(flag_ready, 1)
            any_low = pe.value_load(flag[0:1, 0:1].bitcast(I32), min_val=0, max_val=2**31 - 1)
            with pe.If(any_low != 0):
                tail(True)
            with pe.Else():
                tail(False)

        @block.vector
        def _(dve):
            steps = [0]

            def step(ins):
                steps[0] += 1
                ins.then_inc(vec_step, 1)
                return steps[0]

            def moments(n, g, src):
                for t in range(GT):
                    s = step(nc.vector.bn_stats(stats[:, n, g % 2, t], src[:, t]))
                for t in range(GT):
                    dve.wait_ge(vec_step, s - GT + 1 + t)
                    e = step(nc.vector.bn_aggr(mv[:, n, g, t], stats[:, n, g % 2, t]))
                dve.wait_ge(vec_step, e)

            def normalise(n, g, src, dst, r, done):
                for t in range(GT):
                    ins = nc.vector.tensor_scalar(dst[:, t], src[:, t], mv[:, n, g, t, 0:1], r[:, t:t + 1],
                                                  ALU.subtract, ALU.mult)
                    if t < GT - 1 or done is None:
                        s = step(ins)
                    else:
                        ins.then_inc(done, 1)
                return s

            def ln0(g):
                dve.wait_ge(x_in[g], 16)
                moments(0, g, x[:, g])
                var = mv[:, 0, g, :, 1]
                k = 1.0 / (N_SCALE * N_SCALE)
                step(nc.vector.tensor_scalar(small[:, g], var, EPS, MIN_SQ * k, ALU.add, ALU.mult))
                s = step(nc.vector.tensor_scalar(base0[:, g, GT:2 * GT], var, EPS, None, ALU.add))
                dve.wait_ge(vec_step, s)
                nc.vector.scalar_tensor_tensor(out=base0[:, g, 0:GT], in0=var, scalar=D * k, in1=small[:, g],
                                               op0=ALU.mult, op1=ALU.max).then_inc(base_ready[0], 1)

            def n_rows(g):
                dve.wait_ge(pow_ready[0], g + 1)
                if g >= 2:
                    dve.wait_ge(aT_ready, g - 1)
                normalise(0, g, x[:, g], nrm[:, g % 2], pow0[:, g], nrm_ready)

            def n_low(g):
                dve.wait_ge(n_hi_ready, g + 1)
                c = slice(g * GW, (g + 1) * GW)
                nc.vector.tensor_tensor(n_lo[:, c], (ps_tr, ps_at, ps_tr, ps_tr)[g][:], n_hi[:, c],
                                        ALU.subtract).then_inc(n_lo_ready, 1)

            def column_sums(b, us):
                for u in us:
                    i, half, first, w = units[u]
                    n = b * NU + u
                    skip = P if half == 0 else 0
                    if w == skip:
                        continue
                    dve.wait_ge(relu_done, n + 1)
                    src = relu[:, n % 4, skip:w]
                    dst = acc[:, b, first + skip:first + w]
                    if i == 0:
                        ins = nc.vector.tensor_copy(dst, src)
                    else:
                        dve.wait_ge(acc_done, b * NA + u - half)
                        ins = nc.vector.tensor_tensor(dst, dst, src, ALU.add)
                    ins.then_inc(acc_done, 1)

            def diagonals(b):
                dve.wait_ge(relu_done, (b + 1) * NU)
                dve.wait_ge(acc_done, (b + 1) * NA)
                s = step(nc.vector.tensor_tensor(row[:, b], rows[:, b, 0], rows[:, b, 1], ALU.add))
                dve.wait_ge(vec_step, s)
                for j in range(BT):
                    dst = acc[:, b, j * P:(j + 1) * P]
                    if j == 0:
                        ins = nc.vector.tensor_scalar(dst, ident[:], row[:, b, j:j + 1], None, ALU.mult)
                    else:
                        ins = nc.vector.scalar_tensor_tensor(out=dst, in0=ident[:], scalar=row[:, b, j:j + 1],
                                                             in1=dst, op0=ALU.mult, op1=ALU.add)
                    ins.then_inc(diag_done, 1)

            def softplus_low(g):
                dve.wait_ge(softplus_log, g + 1)
                dve.wait_ge(z_read, g + 1)
                if g >= 2:
                    dve.wait_ge(sp_lo_ready, g - 1)
                nc.vector.tensor_tensor(sp[:, g % 2], z_abs[:, g % 2], z_pos[:, g % 2], ALU.add).then_inc(sp_ready, 1)
                dve.wait_ge(sp_hi_ready, g + 1)
                nc.vector.tensor_tensor(sp_lo[:, g % 2], sp[:, g % 2], sp_hi[:, g % 2],
                                        ALU.subtract).then_inc(sp_lo_ready, 1)

            def scale_data(g):
                dve.wait_ge(pa_ready, g + 1)
                dve.wait_ge(gq_ready, g + 1)
                nc.vector.tensor_tensor(y[:, g % 2], ps_at[:].rearrange("p (t d) -> p t d", t=GT),
                                        gq[:, g].unsqueeze(2).to_broadcast([P, GT, D]), ALU.mult).then_inc(y_done, 1)

            def attn_out(g):
                dve.wait_ge(pb_ready, g + 1)
                dve.wait_ge(y_done, g + 1)
                nc.vector.tensor_tensor(y2[:, g % 2], ps_at[:].rearrange("p (t d) -> p t d", t=GT), y[:, g % 2],
                                        ALU.add).then_inc(y2_done, 1)
                dve.wait_ge(y2_done, g + 1)
                moments(1, g, y2[:, g % 2])
                nc.vector.tensor_scalar(base[:, 0, g], mv[:, 1, g, :, 1], EPS * W_SCALE * W_SCALE, None,
                                        ALU.add).then_inc(base_ready[1], 1)
                dve.wait_ge(pow_ready[1], g + 1)
                s = normalise(1, g, y2[:, g % 2], y[:, g % 2], rstd[:, 0, g], None)
                dve.wait_ge(vec_step, s)
                s = step(nc.vector.tensor_tensor(x1[:, g], x[:, g], y[:, g % 2], ALU.add))
                dve.wait_ge(vec_step, s)
                moments(2, g, x1[:, g])
                nc.vector.tensor_scalar(base[:, 1, g], mv[:, 2, g, :, 1], EPS, None, ALU.add).then_inc(base_ready[2], 1)

            def a_rows(g):
                dve.wait_ge(pow_ready[2], g + 1)
                if g == 0:
                    dve.wait_ge(nT_ready, 2)
                elif g >= 2:
                    dve.wait_ge(nT_ready, 4)
                normalise(2, g, x1[:, g], nrm[:, g % 2], rstd[:, 1, g], a_rows_ready)

            def scaled_low(dst, src, hi, n):
                return nc.vector.tensor_tensor_reduce(dst, src, hi, LO_SCALE, 0.0, ALU.subtract, ALU.max,
                                                      sink[:, n:n + 1])

            def a_low(g):
                dve.wait_ge(a_hi_ready, g + 1)
                scaled_low(a_lo[:, g], ps_tr[:], a_hi[:, g], 2 * G * M + g).then_inc(a_lo_ready, 1)

            def up_gate(g):
                def gate(m):
                    n = M * g + m
                    dve.wait_ge(up_ready, 2 * n + 2)
                    dve.wait_ge(silu_done, n + 1)
                    if n >= 2:
                        dve.wait_ge(up_hi_ready, n - 1)
                        dve.wait_ge(up_lo_ready, n - 1)
                    nc.vector.scalar_tensor_tensor(out=gate_f[:, n % 2], in0=ps_ff[:, 2 * (m % 2) + 1],
                                                   scalar=colk[:, M + m:M + m + 1], in1=act_f[:, n % 4],
                                                   op0=ALU.mult, op1=ALU.mult).then_inc(gate_done, 1)

                def low(m):
                    n = M * g + m
                    dve.wait_ge(up_hi_ready, n + 1)
                    nc.vector.scalar_tensor_tensor(out=ho_lo[:, g % BG, m], in0=ho_hi[:, g % BG, m], scalar=-LO_SCALE,
                                                   in1=gate_f[:, n % 2], op0=ALU.mult,
                                                   op1=ALU.add).then_inc(up_lo_ready, 1)

                gate(0)
                for m in range(1, M):
                    gate(m)
                    low(m - 1)
                low(M - 1)

            def hid_low(layer, g):
                src, dst = ((he_hi, he_lo), (ho_hi, ho_lo))[layer]
                for m in range(M):
                    n = hid_index(layer, g, m)
                    dve.wait_ge(hid_hi_ready, n + 1)
                    scaled_low(dst[:, g % BG, m], act_f[:, n % 4], src[:, g % BG, m], n).then_inc(hid_lo_ready, 1)

            def finish(g):
                dve.wait_ge(down_ready, g + 1)
                if g == 0:
                    dve.wait_ge(s3_in, 16)
                nc.vector.tensor_tensor(y[:, g % 2], ps_ff[:, g % 2].rearrange("p (t d) -> p t d", t=GT),
                                        s3b[:].unsqueeze(1).to_broadcast([P, GT, D]),
                                        ALU.mult).then_inc(down_read, 1)
                dve.wait_ge(down_read, g + 1)
                moments(3, g, y[:, g % 2])
                nc.vector.tensor_scalar(base[:, 2, g], mv[:, 3, g, :, 1], EPS * W_SCALE * W_SCALE, None,
                                        ALU.add).then_inc(base_ready[3], 1)

            def store(g):
                dve.wait_ge(pow_ready[3], g + 1)
                s = normalise(3, g, y[:, g % 2], y2[:, g % 2], rstd[:, 2, g], None)
                dve.wait_ge(vec_step, s)
                nc.vector.tensor_tensor(x1[:, g], x1[:, g], y2[:, g % 2], ALU.add).then_inc(out_ready, 1)

            def weight_scaled(s0, s1):
                dve.wait_ge(w_hi_ready, s1)
                step(nc.vector.tensor_scalar(w_his[:, 512 * s0:512 * s1], w_hi[:, 512 * s0:512 * s1],
                                             1.0 / LO_SCALE, None, ALU.mult))

            ln0(0)
            ln0(1)
            n_rows(0)
            n_rows(1)
            dve.wait_ge(cols_in, 16)
            step(nc.vector.tensor_scalar(colk[:, 0:M], col[:, 0:M], 1.0 / W_SCALE, None, ALU.mult))
            step(nc.vector.tensor_scalar(colk[:, M:2 * M], col[:, M:2 * M], LO_SCALE / W_SCALE, None, ALU.mult))
            step(nc.vector.tensor_scalar(colk[:, 2 * M:4 * M], col[:, 2 * M:4 * M], 1.0 / W_SCALE, None, ALU.mult))
            nc.vector.tensor_scalar(colk[:, 4 * M:4 * M + 1], col[:, 4 * M:4 * M + 1],
                                    1.0 / (N_SCALE * N_SCALE), None, ALU.mult).then_inc(colk_ready, 1)
            n_low(0)
            n_low(1)
            dve.wait_ge(aw_hi_ready, 1)
            nc.vector.scalar_tensor_tensor(out=aw_lo[:], in0=aw[:], scalar=W_SCALE, in1=aw_hi[:], op0=ALU.mult,
                                           op1=ALU.subtract).then_inc(aw_lo_ready, 1)
            column_sums(0, range(0, NU // 2))
            ln0(2)
            column_sums(0, range(NU // 2, NU))
            scale_data(0)
            diagonals(0)
            ln0(3)
            weight_scaled(0, N_UP)
            softplus_low(0)
            softplus_low(1)
            attn_out(0)
            a_rows(0)
            scale_data(1)
            weight_scaled(N_UP, N_UP + N_HID)
            attn_out(1)
            a_low(0)
            a_rows(1)
            weight_scaled(N_UP + N_HID, NS)
            a_low(1)
            n_rows(2)
            n_low(2)
            n_rows(3)
            n_low(3)
            dve.wait_ge(lo_sq_ready, NS)
            nc.vector.tensor_reduce(lo_any[:, 0:1], lo_sq[:], AX.X, ALU.add).then_inc(lo_any_ready, 1)
            dve.wait_ge(lo_all_ready, 1)
            nc.vector.tensor_copy(flag[:], ps_at[0:1, 0:1]).then_inc(flag_ready, 1)
            up_gate(0)
            column_sums(1, range(0, NU // 2))
            up_gate(1)
            column_sums(1, range(NU // 2, NU))
            diagonals(1)
            hid_low(0, 0)
            scale_data(2)
            softplus_low(2)
            softplus_low(3)
            hid_low(0, 1)
            attn_out(2)
            a_rows(2)
            scale_data(3)
            hid_low(1, 0)
            a_low(2)
            attn_out(3)
            hid_low(1, 1)
            a_rows(3)
            a_low(3)
            finish(0)
            store(0)
            up_gate(2)
            finish(1)
            store(1)
            up_gate(3)
            for layer in (0, 1):
                for g in (2, 3):
                    hid_low(layer, g)
            finish(2)
            store(2)
            finish(3)
            store(3)


def kernel(**inputs):
    import numpy as np
    import concourse.bacc as bacc
    from concourse.bass_utils import run_bass_kernel_spmd

    f = {n.removeprefix("L0_"): np.asarray(a) for n, a in inputs.items()}
    tokens = f["attn_data"].reshape(-1, f["attn_data"].shape[-1])
    columns = [f[n].reshape(-1, P).T for n in ("ffn_w1_s", "ffn_w2_s", "ffn_h1_s", "ffn_h2_s", "attn_W1", "attn_b1")]
    arrays = {
        "data": tokens,
        "identity": np.eye(P, dtype=np.float32),
        "cols": np.concatenate(columns, axis=1),
        "attn_w": f["attn_W2"].reshape(2, P, P).transpose(1, 0, 2),
        "up_w": np.concatenate([f["ffn_w1_w"].T, f["ffn_w2_w"].T], axis=1),
        "h1_w": f["ffn_h1_w"].T,
        "h2_w": f["ffn_h2_w"].T,
        "w3_w": f["ffn_w3_w"].T,
        "s3_row": f["ffn_w3_s"],
    }
    arrays = {n: np.ascontiguousarray(a) for n, a in arrays.items()}
    nc = bacc.Bacc("TRN2", target_bir_lowering=False, num_devices=1)
    dram = [nc.dram_tensor(n, a.shape, mybir.dt.from_np(a.dtype), kind="ExternalInput").ap()
            for n, a in arrays.items()]
    out = nc.dram_tensor("out", tokens.shape, F32, kind="ExternalOutput").ap()
    build(nc, *dram, out)
    r = run_bass_kernel_spmd(nc, [arrays], core_ids=[0])
    return r.results[0]["out"].reshape(f["attn_data"].shape)
```

```python
from contextlib import ExitStack

import concourse.bass as bass
from concourse import mybir

ALU = mybir.AluOpType
ACT = mybir.ActivationFunctionType
AX = mybir.AxisListType
F32 = mybir.dt.float32
F16 = mybir.dt.float16
I32 = mybir.dt.int32

P = 128
EPS = 1e-5
MIN_SQ = 1e-12
N_SCALE = 256.0
W_SCALE = 64.0
LO_SCALE = 2048.0
GT = 4
GW = GT * P


def build(nc, data, identity, cols, attn_w, up_w, h1_w, h2_w, w3_w, s3_row, out):
    D = data.shape[1]
    HID = w3_w.shape[0]
    assert D == P
    M = HID // P
    G = data.shape[0] // GW
    BG = 2
    B = G // BG
    BT = BG * GT
    BW = BG * GW

    units = []
    for i in range(BT):
        for half in range(2):
            first = i * P + half * GW
            if first < BW:
                units.append((i, half, first, min(GW, BW - first)))
    NU = len(units)
    NA = NU - 1

    R = 8

    NS = 2 * HID // 512 + 2 * M + M * D // 512

    x_dram = data.rearrange("(g p t) d -> g p t d", p=P, t=GT)
    out_dram = out.rearrange("(g p t) d -> g p t d", p=P, t=GT)

    with ExitStack() as ctx:
        def sb(name, shape, dt=F32):
            return ctx.enter_context(nc.sbuf_tensor(name, shape, dt))

        def sem(name):
            return ctx.enter_context(nc.semaphore(name))

        x = sb("x", [P, G, GT, D])
        x1 = sb("x1", [P, G, GT, D])
        ident = sb("ident", [P, P])
        ones = sb("ones", [P, P])
        neg_half = sb("neg_half", [P, GT])
        col = sb("col", [P, 4 * M + 2])
        colk = sb("colk", [P, 4 * M + 1])
        s3b = sb("s3b", [P, D])
        wf = sb("wf", [P, NS * 512])
        w_hi = sb("w_hi", [P, NS * 512], F16)
        w_his = sb("w_his", [P, NS * 512], F16)
        w_lo = sb("w_lo", [P, NS * 512], F16)
        lo_sq = sb("lo_sq", [P, 6])
        lo_any = sb("lo_any", [P, 1])
        flag = sb("flag", [1, 1])
        aw = sb("aw", [P, 2 * D])
        aw_hi = sb("aw_hi", [P, 2 * D], F16)
        aw_lo = sb("aw_lo", [P, 2 * D], F16)
        stats = sb("stats", [P, 4, 2, GT, 6])
        mv = sb("mv", [P, 4, G, GT, 2])
        base0 = sb("base0", [P, G, 2 * GT])
        small = sb("small", [P, G, GT])
        root0 = sb("root0", [P, G, 2 * GT])
        pow0 = sb("pow0", [P, G, 2 * GT])
        gq = sb("gq", [P, G, GT])
        base = sb("base", [P, 3, G, GT])
        rstd = sb("rstd", [P, 3, G, GT])
        nrm = sb("nrm", [P, G, GT, D])
        neg_mean = sb("neg_mean", [P, 4, G, GT])
        n_hi = sb("n_hi", [P, G * GW], F16)
        n_lo = sb("n_lo", [P, G * GW], F16)
        junk = sb("junk", [P, 2, 1024], F16)
        relu = sb("relu", [P, R, 512])
        rows = sb("rows", [P, B, 2, BT])
        row = sb("row", [P, B, BT])
        acc = sb("acc", [P, BW])
        z_abs = sb("z_abs", [P, 2, GW])
        z_pos = sb("z_pos", [P, 2, GW])
        sp = sb("sp", [P, 2, GW])
        sp_hi = sb("sp_hi", [P, 2, GW], F16)
        sp_lo = sb("sp_lo", [P, 2, GW], F16)
        y = sb("y", [P, 2, GT, D])
        y2 = sb("y2", [P, 2, GT, D])
        a_hi = sb("a_hi", [P, G, GW], F16)
        a_lo = sb("a_lo", [P, G, GW], F16)
        silu_f = sb("silu_f", [P, 2, GW])
        gelu_f = sb("gelu_f", [P, 4, GW])
        gate_f = sb("gate_f", [P, 2, GW])
        ho_hi = sb("ho_hi", [P, BG, M, GW], F16)
        ho_lo = sb("ho_lo", [P, BG, M, GW], F16)
        he_hi = sb("he_hi", [P, BG, M, GW], F16)
        he_lo = sb("he_lo", [P, BG, M, GW], F16)
        sink = sb("sink", [P, 2 * G * M + G])

        ps_row = ctx.enter_context(nc.psum_tensor("ps_row", [P, 2, 512], F32))
        ps_two = ctx.enter_context(nc.psum_tensor("ps_two", [P, 2, 512], F32))
        ps_up = ctx.enter_context(nc.psum_tensor("ps_up", [P, 4, 512], F32))

        x_in = [sem(f"x_in{g}") for g in range(G)]
        ident_in, cols_in, aw_in, s3_in, up_in, h1_in, h2_in, w3_in = (
            sem(n) for n in ("ident_in", "cols_in", "aw_in", "s3_in", "up_in", "h1_in", "h2_in", "w3_in"))
        ones_set = sem("ones_set")
        sums_zeroed = sem("sums_zeroed")
        pool_step = sem("pool_step")
        vec_step = sem("vec_step")
        z_abs_ready = sem("z_abs_ready")
        z_exp_ready = sem("z_exp_ready")
        base_ready = [sem(f"base_ready{n}") for n in range(4)]
        root_ready = sem("root_ready")
        pow0_ready = sem("pow0_ready")
        gq_ready = sem("gq_ready")
        norm_ready = [None] + [sem(f"norm_ready{n}") for n in range(1, 4)]
        n_rows_vec = sem("n_rows_vec")
        n_rows_pool = sem("n_rows_pool")
        nT_ready = sem("nT_ready")
        n_hi_ready = sem("n_hi_ready")
        n_lo_ready = sem("n_lo_ready")
        sim_ready = sem("sim_ready")
        relu_done = sem("relu_done")
        strip_added = sem("strip_added")
        acc_done = sem("acc_done")
        row_ready = sem("row_ready")
        count_ready = sem("count_ready")
        z_read = sem("z_read")
        softplus_log = sem("softplus_log")
        sp_ready = sem("sp_ready")
        sp_hi_ready = sem("sp_hi_ready")
        sp_lo_ready = sem("sp_lo_ready")
        pa_ready = sem("pa_ready")
        pb_ready = sem("pb_ready")
        y_done = sem("y_done")
        y2_done = sem("y2_done")
        aT_ready = sem("aT_ready")
        a_hi_ready = sem("a_hi_ready")
        a_lo_ready = sem("a_lo_ready")
        aw_hi_ready = sem("aw_hi_ready")
        aw_lo_ready = sem("aw_lo_ready")
        w_hi_ready = sem("w_hi_ready")
        w_his_ready = sem("w_his_ready")
        w_lo_ready = sem("w_lo_ready")
        lo_sq_ready = sem("lo_sq_ready")
        lo_any_ready = sem("lo_any_ready")
        lo_all_ready = sem("lo_all_ready")
        flag_ready = sem("flag_ready")
        colk_ready = sem("colk_ready")
        up_ready = sem("up_ready")
        silu_done = sem("silu_done")
        gate_done = sem("gate_done")
        up_hi_ready = sem("up_hi_ready")
        up_lo_ready = sem("up_lo_ready")
        hid_ready = sem("hid_ready")
        gelu_done = sem("gelu_done")
        hid_hi_ready = sem("hid_hi_ready")
        hid_lo_ready = sem("hid_lo_ready")
        down_ready = sem("down_ready")
        down_read = sem("down_read")
        out_ready = sem("out_ready")
        out_stored = sem("out_stored")

        off_up = 0
        off_hid = [2 * HID, 2 * HID + M * HID]
        off_w3 = 2 * HID + 2 * M * HID
        blocks = [(off_up, off_hid[0], up_in), (off_hid[0], off_hid[1], h1_in),
                  (off_hid[1], off_w3, h2_in), (off_w3, off_w3 + M * D, w3_in)]
        parts = [(c, min(1024, c1 - c)) for c0, c1, _ in blocks for c in range(c0, c1, 1024)]

        def hid_index(layer, g, m):
            b, i = divmod(g, BG)
            return ((b * 2 + layer) * BG + i) * M + m

        HU = 2 * BG * M
        BATCH_TURNS = HU + BG
        DOWN_FIRST, DOWN_LAST = HU - 2, HU + 1

        def hid_turn(n):
            b, k = divmod(n, HU)
            return b * BATCH_TURNS + k + (k >= DOWN_FIRST)

        def down_turn(g):
            b, i = divmod(g, BG)
            return b * BATCH_TURNS + (DOWN_FIRST, DOWN_LAST)[i]

        def turn_read(turn):
            b, k = divmod(turn, BATCH_TURNS)
            if k in (DOWN_FIRST, DOWN_LAST):
                return down_read, b * BG + (1 if k == DOWN_FIRST else 2)
            return gelu_done, b * HU + k - (k > DOWN_FIRST) + 1

        UH = sum(i < GT for i, _, _, _ in units)

        def attn_bank(g, second):
            return ps_up[:, 2 * second + g] if g < BG else ps_row[:, g % BG]

        def n_bank(g):
            return ps_row[:, g] if g < BG else ps_up[:, g]

        block = ctx.enter_context(nc.Block())

        @block.sync
        def _(sync):
            sync.dma_start(x[:, 0], x_dram[0]).then_inc(x_in[0], 16)
            sync.dma_start(x[:, 1], x_dram[1]).then_inc(x_in[1], 16)
            sync.dma_start(ident[:], identity).then_inc(ident_in, 16)
            sync.dma_start(aw[:].rearrange("p (k n) -> p k n", k=2), attn_w).then_inc(aw_in, 16)
            sync.dma_start(wf[:, 0:off_hid[0]], up_w).then_inc(up_in, 16)
            sync.dma_start(x[:, 2], x_dram[2]).then_inc(x_in[2], 16)
            sync.dma_start(x[:, 3], x_dram[3]).then_inc(x_in[3], 16)
            sync.dma_start(col[:], cols).then_inc(cols_in, 16)
            for off, w, s in ((off_hid[0], h1_w, h1_in), (off_hid[1], h2_w, h2_in)):
                sync.dma_start(wf[:, off:off + M * HID].rearrange("p (k n) -> p k n", k=M),
                               w.rearrange("(k p) n -> p k n", p=P)).then_inc(s, 16)
            sync.dma_start(wf[:, off_w3:off_w3 + M * D].rearrange("p (k n) -> p k n", k=M),
                           w3_w.rearrange("(k p) n -> p k n", p=P)).then_inc(w3_in, 16)
            sync.dma_start(s3b[:], s3_row.partition_broadcast(P)).then_inc(s3_in, 16)
            for g in range(G):
                sync.wait_ge(out_ready, g + 1)
                sync.dma_start(out_dram[g], x1[:, g]).then_inc(out_stored, 16)
            sync.wait_ge(out_stored, 16 * G)

        @block.gpsimd
        def _(pool):
            steps = [0]

            def step(ins):
                steps[0] += 1
                ins.then_inc(pool_step, 1)
                return steps[0]

            def row_length(g):
                pool.wait_ge(pow0_ready, g + 1)
                s = step(nc.gpsimd.tensor_tensor(gq[:, g], pow0[:, g, 0:GT], pow0[:, g, GT:2 * GT], ALU.mult))
                pool.wait_ge(pool_step, s)
                nc.gpsimd.tensor_tensor(gq[:, g], gq[:, g], base0[:, g, 0:GT], ALU.mult).then_inc(gq_ready, 1)

            def normalise(n, g, src, dst, r, done):
                s = step(nc.gpsimd.tensor_scalar(neg_mean[:, n, g], mv[:, n, g, :, 0], -1.0, 0.0,
                                                 ALU.mult, ALU.add))
                if n:
                    s = step(nc.gpsimd.tensor_tensor(r, base[:, n - 1, g], neg_half[:], ALU.pow))
                pool.wait_ge(pool_step, s)
                for t in range(GT):
                    ins = nc.gpsimd.tensor_scalar(dst[:, t], src[:, t], neg_mean[:, n, g, t:t + 1], r[:, t:t + 1],
                                                  ALU.add, ALU.mult)
                ins.then_inc(done, 1)

            def n_rows(g):
                pool.wait_ge(pow0_ready, g + 1)
                normalise(0, g, x[:, g], nrm[:, g], pow0[:, g, 0:GT], n_rows_pool)

            def norm1(g):
                pool.wait_ge(base_ready[1], g + 1)
                normalise(1, g, y2[:, g % 2], y[:, g % 2], rstd[:, 0, g], norm_ready[1])

            def norm2(g):
                pool.wait_ge(base_ready[2], g + 1)
                pool.wait_ge(nT_ready, g + 1)
                normalise(2, g, x1[:, g], nrm[:, g], rstd[:, 1, g], norm_ready[2])

            def norm3(g):
                pool.wait_ge(base_ready[3], g + 1)
                normalise(3, g, y[:, g % 2], y2[:, g % 2], rstd[:, 2, g], norm_ready[3])

            def result(g):
                pool.wait_ge(norm_ready[3], g + 1)
                nc.gpsimd.tensor_tensor(x1[:, g], x1[:, g], y2[:, g % 2], ALU.add).then_inc(out_ready, 1)

            def softplus_hi(g):
                pool.wait_ge(sp_ready, g + 1)
                nc.gpsimd.tensor_scalar(sp_hi[:, g % 2], sp[:, g % 2], 1.0, 0.0,
                                        ALU.mult, ALU.add).then_inc(sp_hi_ready, 1)

            def up_hi(g):
                for m in range(M):
                    n = M * g + m
                    pool.wait_ge(gate_done, n + 1)
                    nc.gpsimd.tensor_scalar(ho_hi[:, g % BG, m], gate_f[:, n % 2], 1.0 / LO_SCALE, 0.0,
                                            ALU.mult, ALU.add).then_inc(up_hi_ready, 1)

            nc.gpsimd.memset(ones[:], 1.0).then_inc(ones_set, 1)
            nc.gpsimd.memset(rows[:], 0.0).then_inc(sums_zeroed, 1)
            nc.gpsimd.memset(acc[:, 0:P], 0.0).then_inc(sums_zeroed, 1)
            pool.wait_ge(pool_step, step(nc.gpsimd.memset(neg_half[:], -0.5)))
            n_rows(1)
            row_length(0)
            n_rows(2)
            n_rows(3)
            row_length(1)
            row_length(2)
            row_length(3)
            softplus_hi(0)
            softplus_hi(1)
            norm1(0)
            norm1(1)
            norm2(0)
            norm2(1)
            softplus_hi(2)
            softplus_hi(3)
            up_hi(0)
            up_hi(1)
            norm1(2)
            norm1(3)
            norm2(2)
            norm2(3)
            norm3(0)
            result(0)
            up_hi(2)
            norm3(1)
            result(1)
            up_hi(3)
            norm3(2)
            norm3(3)

        @block.scalar
        def _(act):
            def root(g):
                act.wait_ge(base_ready[0], g + 1)
                nc.scalar.activation(root0[:, g], base0[:, g], ACT.Sqrt).then_inc(root_ready, 1)

            def squares(i):
                c, w = parts[i]
                act.wait_ge(w_lo_ready, i + 1)
                if i >= 2:
                    act.wait_ge(lo_sq_ready, i - 1)
                nc.scalar.activation(junk[:, i % 2, 0:w], w_lo[:, c:c + w], ACT.Square,
                                     accum_out=lo_sq[:, i:i + 1]).then_inc(lo_sq_ready, 1)

            def n_high(g):
                act.wait_ge(nT_ready, g + 1)
                nc.scalar.copy(n_hi[:, g * GW:(g + 1) * GW], n_bank(g)).then_inc(n_hi_ready, 1)

            def relu_sums(b, us):
                for u in us:
                    i, half, _, w = units[u]
                    n = b * NU + u
                    act.wait_ge(sim_ready, n + 1)
                    if n >= R:
                        act.wait_ge(relu_done, n - R + 1)
                        if n < NU + R:
                            act.wait_ge(acc_done, min(n - R + 1, NA))
                        else:
                            act.wait_ge(strip_added, n - NU - R + 1)
                    elif n == 0:
                        act.wait_ge(sums_zeroed, 1)
                    nc.scalar.activation(relu[:, n % R, 0:w], ps_two[:, n % 2, 0:w], ACT.Relu,
                                         accum_out=rows[:, b, half, i:i + 1]).then_inc(relu_done, 1)

            def softplus_z(g):
                act.wait_ge(count_ready, g + 1)
                act.wait_ge(colk_ready, 1)
                if g >= 2:
                    act.wait_ge(sp_ready, g - 1)
                w1c, b1c = colk[:, 4 * M:4 * M + 1], col[:, 4 * M + 1:4 * M + 2]
                nc.scalar.activation(z_abs[:, g % 2], ps_row[:, g % 2], ACT.Abs, bias=b1c,
                                     scale=w1c).then_inc(z_abs_ready, 1)
                nc.scalar.activation(z_pos[:, g % 2], ps_row[:, g % 2], ACT.Relu, bias=b1c,
                                     scale=w1c).then_inc(z_read, 1)

            def softplus_ln(g):
                z = z_abs[:, g % 2]
                act.wait_ge(z_abs_ready, g + 1)
                nc.scalar.activation(z, z, ACT.Exp, scale=-1.0).then_inc(z_exp_ready, 1)
                act.wait_ge(z_exp_ready, g + 1)
                nc.scalar.activation(z, z, ACT.Ln, bias=1.0).then_inc(softplus_log, 1)

            def a_high(g):
                act.wait_ge(aT_ready, g + 1)
                nc.scalar.copy(a_hi[:, g], ps_row[:, g % 2]).then_inc(a_hi_ready, 1)

            def silu(g):
                for m in range(M):
                    n = M * g + m
                    act.wait_ge(up_ready, 2 * n + 1)
                    if n >= 2:
                        act.wait_ge(gate_done, n - 1)
                    nc.scalar.activation(silu_f[:, n % 2], ps_up[:, 2 * (m % 2)], ACT.Silu,
                                         scale=colk[:, m:m + 1]).then_inc(silu_done, 1)

            def gelu(layer, g):
                dst = (he_hi, ho_hi)[layer]
                scale = colk[:, (2 + layer) * M:(3 + layer) * M]
                for m in range(M):
                    n = hid_index(layer, g, m)
                    src = ps_two[:, hid_turn(n) % 2]
                    act.wait_ge(hid_ready, n + 1)
                    nc.scalar.activation(dst[:, g % BG, m], src, ACT.Gelu,
                                         scale=scale[:, m:m + 1]).then_inc(hid_hi_ready, 1)
                    if n >= 4:
                        act.wait_ge(hid_lo_ready, n - 3)
                    nc.scalar.activation(gelu_f[:, n % 4], src, ACT.Gelu,
                                         scale=scale[:, m:m + 1]).then_inc(gelu_done, 1)

            root(0)
            root(1)
            n_high(0)
            root(2)
            n_high(1)
            root(3)
            nc.scalar.preload_act_table_set("natural_log_exp_and_others")
            act.wait_ge(aw_in, 16)
            nc.scalar.activation(aw_hi[:], aw[:], ACT.Copy, scale=W_SCALE).then_inc(aw_hi_ready, 1)
            relu_sums(0, range(0, 4))
            n_high(2)
            n_high(3)
            relu_sums(0, range(4, NU))
            relu_sums(1, [0])
            softplus_z(0)
            relu_sums(1, [1])
            softplus_ln(0)
            relu_sums(1, [2])
            softplus_z(1)
            relu_sums(1, [3])
            softplus_ln(1)
            relu_sums(1, [4, 5])
            for i, us in enumerate(([6], [7], [8], range(9, NU))):
                squares(i)
                relu_sums(1, us)
            softplus_z(2)
            softplus_z(3)
            softplus_ln(2)
            softplus_ln(3)
            squares(4)
            squares(5)
            a_high(0)
            nc.scalar.preload_act_table_set("silu_and_others")
            a_high(1)
            silu(0)
            silu(1)
            gelu(0, 0)
            gelu(0, 1)
            gelu(1, 0)
            a_high(2)
            gelu(1, 1)
            a_high(3)
            silu(2)
            silu(3)
            for layer in (0, 1):
                for g in (2, 3):
                    gelu(layer, g)

        @block.tensor
        def _(pe):
            def n_transpose(g):
                if g == 0:
                    pe.wait_ge(ident_in, 16)
                    pe.wait_ge(n_rows_vec, 1)
                else:
                    pe.wait_ge(n_rows_pool, g)
                for t in range(GT):
                    mm = nc.tensor.transpose(n_bank(g)[:, t * P:(t + 1) * P], nrm[:, g, t], ident[:])
                mm.then_inc(nT_ready, 1)

            def similarity(b, us):
                for u in us:
                    i, _, first, w = units[u]
                    n = b * NU + u
                    if u <= 1:
                        pe.wait_ge(n_lo_ready, BG * b + u + 1)
                    if n >= 2:
                        pe.wait_ge(relu_done, n - 1)
                    r = b * BW + i * P
                    c = b * BW + first
                    dst = ps_two[:, n % 2, 0:w]
                    nc.tensor.matmul(dst, n_hi[:, r:r + P], n_hi[:, c:c + w], start=True, stop=False)
                    nc.tensor.matmul(dst, n_hi[:, r:r + P], n_lo[:, c:c + w], start=False, stop=False)
                    nc.tensor.matmul(dst, n_lo[:, r:r + P], n_hi[:, c:c + w], start=False,
                                     stop=True).then_inc(sim_ready, 1)

            def strip_sums(us):
                for u in us:
                    i, half, first, w = units[u]
                    n = NU + u
                    skip = P if half == 0 else 0
                    pe.wait_ge(relu_done, n + 1)
                    if u == 0:
                        pe.wait_ge(z_read, BG)
                    c0, c1 = first + skip, first + w
                    for h in range(BG):
                        a, b = max(c0, h * GW), min(c1, (h + 1) * GW)
                        if a < b:
                            mm = nc.tensor.matmul(ps_row[:, h, a - h * GW:b - h * GW], ones[:],
                                                  relu[:, n % R, a - first:b - first], start=(i == 0), stop=False)
                    mm.then_inc(strip_added, 1)

            def counter(g):
                b, i = divmod(g, BG)
                dst = ps_row[:, g % 2]
                if b == 0:
                    if g == 0:
                        pe.wait_ge(ones_set, 1)
                        pe.wait_ge(sums_zeroed, 2)
                    pe.wait_ge(acc_done, (UH, NA)[i])
                    nc.tensor.matmul(dst, ones[:], acc[:, i * GW:(i + 1) * GW], start=True, stop=False)
                pe.wait_ge(row_ready, g + 1)
                for t in range(GT):
                    j = i * GT + t
                    mm = nc.tensor.matmul(dst[:, t * P:(t + 1) * P], row[:, b, j:j + 1].to_broadcast([P, P]),
                                          ident[:], start=False, stop=(t == GT - 1))
                mm.then_inc(count_ready, 1)

            def row_product(dst, hi, lo, w):
                for t in range(GT):
                    o = dst[:, t * P:(t + 1) * P]
                    c = slice(t * P, (t + 1) * P)
                    nc.tensor.matmul(o, hi[:, c], aw_hi[:, w], start=True, stop=False)
                    nc.tensor.matmul(o, hi[:, c], aw_lo[:, w], start=False, stop=False)
                    mm = nc.tensor.matmul(o, lo[:, c], aw_hi[:, w], start=False, stop=True)
                return mm

            def attn_data(g):
                if g == 0:
                    pe.wait_ge(aw_lo_ready, 1)
                pe.wait_ge(n_lo_ready, g + 1)
                if g >= BG:
                    pe.wait_ge(a_lo_ready, g - 1)
                c = slice(g * GW, (g + 1) * GW)
                row_product(attn_bank(g, 0), n_hi[:, c], n_lo[:, c], slice(0, D)).then_inc(pa_ready, 1)

            def attn_counter(g):
                pe.wait_ge(sp_hi_ready, g + 1)
                pe.wait_ge(sp_lo_ready, g + 1)
                if g < BG:
                    pe.wait_ge(n_lo_ready, g + 3)
                else:
                    pe.wait_ge(y_done, g + 1)
                row_product(attn_bank(g, 1), sp_hi[:, g % 2], sp_lo[:, g % 2],
                            slice(D, 2 * D)).then_inc(pb_ready, 1)

            def a_transpose(g):
                pe.wait_ge(norm_ready[2], g + 1)
                if g < BG:
                    pe.wait_ge(z_read, g + 3)
                else:
                    pe.wait_ge(y2_done, g + 1)
                for t in range(GT):
                    mm = nc.tensor.transpose(ps_row[:, g % 2, t * P:(t + 1) * P], nrm[:, g, t], ident[:])
                mm.then_inc(aT_ready, 1)

            def product(dst, w_col, hi, lo, first, last, general):
                w = slice(w_col, w_col + P)
                nc.tensor.matmul(dst, w_hi[:, w], hi, start=first, stop=False)
                if general:
                    nc.tensor.matmul(dst, w_lo[:, w], hi, start=False, stop=False)
                return nc.tensor.matmul(dst, w_his[:, w], lo, start=False, stop=last)

            def up(g, general):
                pe.wait_ge(a_hi_ready, g + 1)
                pe.wait_ge(a_lo_ready, g + 1)
                for m in range(M):
                    n = M * g + m
                    if n == 0:
                        pe.wait_ge(y_done, BG)
                    elif n == 1:
                        pe.wait_ge(y2_done, BG)
                    else:
                        pe.wait_ge(gate_done, n - 1)
                    for j in range(2):
                        product(ps_up[:, 2 * (m % 2) + j], off_up + j * HID + m * P, a_hi[:, g], a_lo[:, g],
                                True, True, general).then_inc(up_ready, 1)

            def hidden(layer, g, general, ms=range(M)):
                src_hi, src_lo = ((ho_hi, ho_lo), (he_hi, he_lo))[layer]
                for m in ms:
                    n = hid_index(layer, g, m)
                    turn = hid_turn(n)
                    if turn >= 2:
                        pe.wait_ge(*turn_read(turn - 2))
                    else:
                        pe.wait_ge(relu_done, B * NU)
                    if turn == 0:
                        pe.wait_ge(flag_ready, 1)
                    for k in range(M):
                        if m == 0 and layer == 0:
                            pe.wait_ge(up_hi_ready, M * g + k + 1)
                            pe.wait_ge(up_lo_ready, M * g + k + 1)
                        elif m == 0:
                            pe.wait_ge(hid_hi_ready, hid_index(0, g, k) + 1)
                            pe.wait_ge(hid_lo_ready, hid_index(0, g, k) + 1)
                        mm = product(ps_two[:, turn % 2], off_hid[layer] + k * HID + m * P, src_hi[:, g % BG, k],
                                     src_lo[:, g % BG, k], k == 0, k == M - 1, general)
                    mm.then_inc(hid_ready, 1)

            def down(g, general):
                turn = down_turn(g)
                pe.wait_ge(*turn_read(turn - 2))
                for k in range(M):
                    pe.wait_ge(hid_hi_ready, hid_index(1, g, k) + 1)
                    pe.wait_ge(hid_lo_ready, hid_index(1, g, k) + 1)
                    w = slice(off_w3 + k * D, off_w3 + (k + 1) * D)
                    for t in range(GT):
                        o = ps_two[:, turn % 2, t * P:(t + 1) * P]
                        c = slice(t * P, (t + 1) * P)
                        hi, lo = ho_hi[:, g % BG, k, c], ho_lo[:, g % BG, k, c]
                        nc.tensor.matmul(o, hi, w_hi[:, w], start=(k == 0 and t == 0), stop=False)
                        if general:
                            nc.tensor.matmul(o, hi, w_lo[:, w], start=False, stop=False)
                        mm = nc.tensor.matmul(o, lo, w_his[:, w], start=False,
                                              stop=(k == M - 1 and t == GT - 1))
                mm.then_inc(down_ready, 1)

            def flag_total():
                pe.wait_ge(lo_any_ready, 1)
                pe.wait_ge(relu_done, B * NU - 1)
                nc.tensor.matmul(ps_two[0:1, 0, 0:2], lo_any[:], ones[:, 0:2], start=True,
                                 stop=True).then_inc(lo_all_ready, 1)

            def flag_value():
                pe.wait_ge(flag_ready, 1)
                return pe.value_load(flag[0:1, 0:1].bitcast(I32), min_val=0, max_val=2**31 - 1)

            def gated_ffn(general):
                up(0, general)
                attn_data(2)
                up(1, general)
                hidden(0, 0, general)
                attn_counter(2)
                attn_data(3)
                hidden(0, 1, general)
                attn_counter(3)
                hidden(1, 0, general)
                a_transpose(2)
                hidden(1, 1, general, range(0, 2))
                down(0, general)
                hidden(1, 1, general, range(2, M))
                a_transpose(3)
                up(2, general)
                down(1, general)
                up(3, general)
                hidden(0, 2, general)
                hidden(0, 3, general)
                hidden(1, 2, general)
                hidden(1, 3, general, range(0, 2))
                down(2, general)
                hidden(1, 3, general, range(2, M))
                down(3, general)

            n_transpose(0)
            n_transpose(1)
            similarity(0, range(0, 4))
            n_transpose(2)
            n_transpose(3)
            similarity(0, range(4, NU))
            counter(0)
            attn_data(0)
            similarity(1, [0])
            attn_data(1)
            counter(1)
            similarity(1, range(1, 4))
            for u in range(4, NU):
                similarity(1, [u])
                strip_sums([u - 4])
                if u == 5:
                    attn_counter(0)
                if u == 7:
                    attn_counter(1)
            strip_sums(range(NU - 4, NA))
            counter(2)
            counter(3)
            flag_total()
            a_transpose(0)
            a_transpose(1)
            pe.wait_ge(w_hi_ready, len(blocks))
            pe.wait_ge(w_his_ready, len(blocks))
            with pe.If(flag_value() != 0):
                gated_ffn(True)
            with pe.Else():
                gated_ffn(False)

        @block.vector
        def _(dve):
            steps = [0]

            def step(ins):
                steps[0] += 1
                ins.then_inc(vec_step, 1)
                return steps[0]

            def moments(n, g, src):
                for t in range(GT):
                    s = step(nc.vector.bn_stats(stats[:, n, g % 2, t], src[:, t]))
                for t in range(GT):
                    dve.wait_ge(vec_step, s - GT + 1 + t)
                    e = step(nc.vector.bn_aggr(mv[:, n, g, t], stats[:, n, g % 2, t]))
                dve.wait_ge(vec_step, e)

            def moments_plus(n, g, src, eps):
                moments(n, g, src)
                nc.vector.tensor_scalar(base[:, n - 1, g], mv[:, n, g, :, 1], eps, None,
                                        ALU.add).then_inc(base_ready[n], 1)

            def ln0(g):
                dve.wait_ge(x_in[g], 16)
                moments(0, g, x[:, g])
                var = mv[:, 0, g, :, 1]
                k = 1.0 / (N_SCALE * N_SCALE)
                step(nc.vector.tensor_scalar(small[:, g], var, EPS, MIN_SQ * k, ALU.add, ALU.mult))
                s = step(nc.vector.tensor_scalar(base0[:, g, GT:2 * GT], var, EPS, None, ALU.add))
                dve.wait_ge(vec_step, s)
                nc.vector.scalar_tensor_tensor(out=base0[:, g, 0:GT], in0=var, scalar=D * k, in1=small[:, g],
                                               op0=ALU.mult, op1=ALU.max).then_inc(base_ready[0], 1)

            def inverse_root(g):
                dve.wait_ge(root_ready, g + 1)
                nc.vector.reciprocal(pow0[:, g], root0[:, g]).then_inc(pow0_ready, 1)

            def n_rows(g):
                dve.wait_ge(pow0_ready, g + 1)
                for t in range(GT):
                    ins = nc.vector.tensor_scalar(nrm[:, g, t], x[:, g, t], mv[:, 0, g, t, 0:1],
                                                  pow0[:, g, t:t + 1], ALU.subtract, ALU.mult)
                ins.then_inc(n_rows_vec, 1)

            def n_low(g):
                dve.wait_ge(n_hi_ready, g + 1)
                c = slice(g * GW, (g + 1) * GW)
                nc.vector.tensor_tensor(n_lo[:, c], n_bank(g), n_hi[:, c], ALU.subtract).then_inc(n_lo_ready, 1)

            def column_sums(us):
                for u in us:
                    i, half, first, w = units[u]
                    skip = P if half == 0 else 0
                    if w == skip:
                        continue
                    dve.wait_ge(relu_done, u + 1)
                    src = relu[:, u % R, skip:w]
                    dst = acc[:, first + skip:first + w]
                    if i == 0:
                        ins = nc.vector.tensor_copy(dst, src)
                    else:
                        dve.wait_ge(acc_done, u - half)
                        ins = nc.vector.tensor_tensor(dst, dst, src, ALU.add)
                    ins.then_inc(acc_done, 1)

            def row_sums(g):
                b, i = divmod(g, BG)
                dve.wait_ge(relu_done, b * NU + (UH, NU)[i])
                c = slice(i * GT, (i + 1) * GT)
                nc.vector.tensor_tensor(row[:, b, c], rows[:, b, 0, c], rows[:, b, 1, c],
                                        ALU.add).then_inc(row_ready, 1)

            def softplus_sum(g):
                dve.wait_ge(softplus_log, g + 1)
                dve.wait_ge(z_read, g + 1)
                if g >= 2:
                    dve.wait_ge(sp_lo_ready, g - 1)
                nc.vector.tensor_tensor(sp[:, g % 2], z_abs[:, g % 2], z_pos[:, g % 2], ALU.add).then_inc(sp_ready, 1)

            def softplus_low(g):
                dve.wait_ge(sp_hi_ready, g + 1)
                nc.vector.tensor_tensor(sp_lo[:, g % 2], sp[:, g % 2], sp_hi[:, g % 2],
                                        ALU.subtract).then_inc(sp_lo_ready, 1)

            def scale_data(g):
                dve.wait_ge(pa_ready, g + 1)
                dve.wait_ge(gq_ready, g + 1)
                nc.vector.tensor_tensor(y[:, g % 2], attn_bank(g, 0).rearrange("p (t d) -> p t d", t=GT),
                                        gq[:, g].unsqueeze(2).to_broadcast([P, GT, D]), ALU.mult).then_inc(y_done, 1)

            def attn_out(g):
                dve.wait_ge(pb_ready, g + 1)
                dve.wait_ge(y_done, g + 1)
                nc.vector.tensor_tensor(y2[:, g % 2], attn_bank(g, 1).rearrange("p (t d) -> p t d", t=GT),
                                        y[:, g % 2], ALU.add).then_inc(y2_done, 1)
                dve.wait_ge(y2_done, g + 1)
                moments_plus(1, g, y2[:, g % 2], EPS * W_SCALE * W_SCALE)

            def residual(g):
                dve.wait_ge(norm_ready[1], g + 1)
                s = step(nc.vector.tensor_tensor(x1[:, g], x[:, g], y[:, g % 2], ALU.add))
                dve.wait_ge(vec_step, s)
                moments_plus(2, g, x1[:, g], EPS)

            def scaled_low(dst, src, hi, n):
                return nc.vector.tensor_tensor_reduce(dst, src, hi, LO_SCALE, 0.0, ALU.subtract, ALU.max,
                                                      sink[:, n:n + 1])

            def a_low(g):
                dve.wait_ge(a_hi_ready, g + 1)
                scaled_low(a_lo[:, g], ps_row[:, g % 2], a_hi[:, g], 2 * G * M + g).then_inc(a_lo_ready, 1)

            def up_gate(g):
                def gate(m):
                    n = M * g + m
                    dve.wait_ge(up_ready, 2 * n + 2)
                    dve.wait_ge(silu_done, n + 1)
                    if n >= 2:
                        dve.wait_ge(up_hi_ready, n - 1)
                        dve.wait_ge(up_lo_ready, n - 1)
                    nc.vector.scalar_tensor_tensor(out=gate_f[:, n % 2], in0=ps_up[:, 2 * (m % 2) + 1],
                                                   scalar=colk[:, M + m:M + m + 1], in1=silu_f[:, n % 2],
                                                   op0=ALU.mult, op1=ALU.mult).then_inc(gate_done, 1)

                def low(m):
                    n = M * g + m
                    dve.wait_ge(up_hi_ready, n + 1)
                    nc.vector.scalar_tensor_tensor(out=ho_lo[:, g % BG, m], in0=ho_hi[:, g % BG, m],
                                                   scalar=-LO_SCALE, in1=gate_f[:, n % 2], op0=ALU.mult,
                                                   op1=ALU.add).then_inc(up_lo_ready, 1)

                gate(0)
                for m in range(1, M):
                    gate(m)
                    low(m - 1)
                low(M - 1)

            def hid_low(layer, g, ms=range(M)):
                src, dst = ((he_hi, he_lo), (ho_hi, ho_lo))[layer]
                for m in ms:
                    n = hid_index(layer, g, m)
                    dve.wait_ge(gelu_done, n + 1)
                    scaled_low(dst[:, g % BG, m], gelu_f[:, n % 4], src[:, g % BG, m], n).then_inc(hid_lo_ready, 1)

            def ffn_out(g):
                dve.wait_ge(down_ready, g + 1)
                if g == 0:
                    dve.wait_ge(s3_in, 16)
                nc.vector.tensor_tensor(y[:, g % 2], ps_two[:, down_turn(g) % 2].rearrange("p (t d) -> p t d", t=GT),
                                        s3b[:].unsqueeze(1).to_broadcast([P, GT, D]),
                                        ALU.mult).then_inc(down_read, 1)
                dve.wait_ge(down_read, g + 1)
                moments_plus(3, g, y[:, g % 2], EPS * W_SCALE * W_SCALE)

            def result(g):
                dve.wait_ge(norm_ready[3], g + 1)
                nc.vector.tensor_tensor(x1[:, g], x1[:, g], y2[:, g % 2], ALU.add).then_inc(out_ready, 1)

            def weights_high(n):
                c0, c1, loaded = blocks[n]
                dve.wait_ge(loaded, 16)
                nc.vector.tensor_scalar(w_hi[:, c0:c1], wf[:, c0:c1], W_SCALE, None, ALU.mult).then_inc(w_hi_ready, 1)
                dve.wait_ge(w_hi_ready, n + 1)
                nc.vector.tensor_scalar(w_his[:, c0:c1], w_hi[:, c0:c1], 1.0 / LO_SCALE, None,
                                        ALU.mult).then_inc(w_his_ready, 1)

            def weights_low(i):
                c, w = parts[i]
                nc.vector.scalar_tensor_tensor(out=w_lo[:, c:c + w], in0=wf[:, c:c + w], scalar=W_SCALE,
                                               in1=w_hi[:, c:c + w], op0=ALU.mult,
                                               op1=ALU.subtract).then_inc(w_lo_ready, 1)

            def flag_sum():
                dve.wait_ge(lo_sq_ready, len(parts))
                nc.vector.tensor_reduce(lo_any[:], lo_sq[:, 0:len(parts)], AX.X, ALU.add).then_inc(lo_any_ready, 1)

            def flag_out():
                dve.wait_ge(lo_all_ready, 1)
                nc.vector.tensor_copy(flag[:], ps_two[0:1, 0, 0:1]).then_inc(flag_ready, 1)

            ln0(0)
            ln0(1)
            inverse_root(0)
            n_rows(0)
            inverse_root(1)
            ln0(2)
            n_low(0)
            inverse_root(2)
            n_low(1)
            ln0(3)
            inverse_root(3)
            dve.wait_ge(cols_in, 16)
            step(nc.vector.tensor_scalar(colk[:, 0:M], col[:, 0:M], 1.0 / W_SCALE, None, ALU.mult))
            step(nc.vector.tensor_scalar(colk[:, M:2 * M], col[:, M:2 * M], LO_SCALE / W_SCALE, None, ALU.mult))
            step(nc.vector.tensor_scalar(colk[:, 2 * M:4 * M], col[:, 2 * M:4 * M], 1.0 / W_SCALE, None, ALU.mult))
            nc.vector.tensor_scalar(colk[:, 4 * M:4 * M + 1], col[:, 4 * M:4 * M + 1],
                                    1.0 / (N_SCALE * N_SCALE), None, ALU.mult).then_inc(colk_ready, 1)
            weights_high(0)
            column_sums(range(0, 2))
            dve.wait_ge(aw_hi_ready, 1)
            nc.vector.scalar_tensor_tensor(out=aw_lo[:], in0=aw[:], scalar=W_SCALE, in1=aw_hi[:], op0=ALU.mult,
                                           op1=ALU.subtract).then_inc(aw_lo_ready, 1)
            column_sums(range(2, 4))
            weights_high(1)
            column_sums(range(4, 6))
            n_low(2)
            n_low(3)
            column_sums(range(6, UH))
            row_sums(0)
            weights_low(0)
            column_sums(range(UH, NU))
            row_sums(1)
            weights_low(1)
            scale_data(0)
            softplus_sum(0)
            weights_low(2)
            softplus_low(0)
            scale_data(1)
            softplus_sum(1)
            weights_high(2)
            softplus_low(1)
            weights_low(3)
            attn_out(0)
            attn_out(1)
            weights_high(3)
            residual(0)
            row_sums(2)
            weights_low(4)
            residual(1)
            row_sums(3)
            weights_low(5)
            flag_sum()
            softplus_sum(2)
            flag_out()
            softplus_sum(3)
            a_low(0)
            softplus_low(2)
            a_low(1)
            softplus_low(3)
            up_gate(0)
            scale_data(2)
            up_gate(1)
            hid_low(0, 0)
            attn_out(2)
            scale_data(3)
            hid_low(0, 1, range(0, 2))
            residual(2)
            hid_low(0, 1, range(2, M))
            attn_out(3)
            hid_low(1, 0, range(0, 2))
            residual(3)
            hid_low(1, 0, range(2, M))
            a_low(2)
            hid_low(1, 1, range(0, 2))
            ffn_out(0)
            hid_low(1, 1, range(2, M))
            a_low(3)
            up_gate(2)
            ffn_out(1)
            up_gate(3)
            hid_low(0, 2)
            hid_low(0, 3)
            hid_low(1, 2)
            hid_low(1, 3, range(0, 2))
            ffn_out(2)
            hid_low(1, 3, range(2, M))
            result(2)
            ffn_out(3)
            result(3)


def kernel(**inputs):
    import numpy as np
    import concourse.bacc as bacc
    from concourse.bass_utils import run_bass_kernel_spmd

    f = {n.removeprefix("L0_"): np.asarray(a) for n, a in inputs.items()}
    tokens = f["attn_data"].reshape(-1, f["attn_data"].shape[-1])
    columns = [f[n].reshape(-1, P).T for n in ("ffn_w1_s", "ffn_w2_s", "ffn_h1_s", "ffn_h2_s", "attn_W1", "attn_b1")]
    arrays = {
        "data": tokens,
        "identity": np.eye(P, dtype=np.float32),
        "cols": np.concatenate(columns, axis=1),
        "attn_w": f["attn_W2"].reshape(2, P, P).transpose(1, 0, 2),
        "up_w": np.concatenate([f["ffn_w1_w"].T, f["ffn_w2_w"].T], axis=1),
        "h1_w": f["ffn_h1_w"].T,
        "h2_w": f["ffn_h2_w"].T,
        "w3_w": f["ffn_w3_w"].T,
        "s3_row": f["ffn_w3_s"],
    }
    arrays = {n: np.ascontiguousarray(a) for n, a in arrays.items()}
    nc = bacc.Bacc("TRN2", target_bir_lowering=False, num_devices=1)
    dram = [nc.dram_tensor(n, a.shape, mybir.dt.from_np(a.dtype), kind="ExternalInput").ap()
            for n, a in arrays.items()]
    out = nc.dram_tensor("out", tokens.shape, F32, kind="ExternalOutput").ap()
    build(nc, *dram, out)
    r = run_bass_kernel_spmd(nc, [arrays], core_ids=[0])
    return r.results[0]["out"].reshape(f["attn_data"].shape)
```

```python
from contextlib import ExitStack

import concourse.bass as bass
from concourse import mybir

ALU = mybir.AluOpType
ACT = mybir.ActivationFunctionType
AX = mybir.AxisListType
F32 = mybir.dt.float32
F16 = mybir.dt.float16
I32 = mybir.dt.int32

P = 128
EPS = 1e-5
MIN_SQ = 1e-12
N_SCALE = 256.0
W_SCALE = 64.0
LO_SCALE = 2048.0
WARM_UP = 16
GT = 4
GW = GT * P


def build(nc, data, identity, cols, attn_w, up_w, h1_w, h2_w, w3_w, s3_row, out):
    D = data.shape[1]
    HID = w3_w.shape[0]
    assert D == P
    M = HID // P
    G = data.shape[0] // GW
    BG = 2
    B = G // BG
    BT = BG * GT
    BW = BG * GW

    units = [(i * GT + t, h) for i in range(BG) for h in range(BG) for t in range(GT)]
    NU = len(units)
    UH = NU // BG

    NS = 2 * HID // 512 + 2 * M + M * D // 512

    x_dram = data.rearrange("(g p t) d -> g p t d", p=P, t=GT)
    out_dram = out.rearrange("(g p t) d -> g p t d", p=P, t=GT)

    with ExitStack() as ctx:
        def sb(name, shape, dt=F32):
            return ctx.enter_context(nc.sbuf_tensor(name, shape, dt))

        def sem(name):
            return ctx.enter_context(nc.semaphore(name))

        x = sb("x", [P, G, GT, D])
        x1 = sb("x1", [P, G, GT, D])
        ident = sb("ident", [P, P])
        ones = sb("ones", [P, P])
        neg_half = sb("neg_half", [P, 2 * GT])
        warm = sb("warm", [P, 512], F16)
        col = sb("col", [P, 4 * M + 2])
        colk = sb("colk", [P, 4 * M + 1])
        s3b = sb("s3b", [P, D])
        wf = sb("wf", [P, NS * 512])
        w_hi = sb("w_hi", [P, NS * 512], F16)
        w_his = sb("w_his", [P, NS * 512], F16)
        w_lo = sb("w_lo", [P, NS * 512], F16)
        lo_sq = sb("lo_sq", [P, 6])
        lo_any = sb("lo_any", [P, 2])
        flag = sb("flag", [1, 2])
        aw = sb("aw", [P, 2 * D])
        aw_hi = sb("aw_hi", [P, 2 * D], F16)
        aw_lo = sb("aw_lo", [P, 2 * D], F16)
        stats = sb("stats", [P, 4, 2, GT, 6])
        mv = sb("mv", [P, 4, G, GT, 2])
        base0 = sb("base0", [P, G, 2 * GT])
        small = sb("small", [P, G, GT])
        root0 = sb("root0", [P, G, 2 * GT])
        pow0 = sb("pow0", [P, G, 2 * GT])
        root3 = sb("root3", [P, GT])
        gq = sb("gq", [P, G, GT])
        base = sb("base", [P, 3, G, GT])
        rstd = sb("rstd", [P, 3, G, GT])
        nrm = sb("nrm", [P, G, GT, D])
        neg_mean = sb("neg_mean", [P, 4, G, GT])
        n_hi = sb("n_hi", [P, G * GW], F16)
        n_lo = sb("n_lo", [P, G * GW], F16)
        lo_sink = sb("lo_sink", [P, 2, 1024], F16)
        relu_sink = sb("relu_sink", [P, 2, 512])
        rows = sb("rows", [P, B, BG, BT])
        row = sb("row", [P, B, BT])
        z_abs = sb("z_abs", [P, 2, GW])
        z_pos = sb("z_pos", [P, 2, GW])
        sp = sb("sp", [P, 2, GW])
        sp_hi = sb("sp_hi", [P, 2, GW], F16)
        sp_lo = sb("sp_lo", [P, 2, GW], F16)
        y = sb("y", [P, 2, GT, D])
        y2 = sb("y2", [P, 2, GT, D])
        a_hi = sb("a_hi", [P, G, GW], F16)
        a_lo = sb("a_lo", [P, G, GW], F16)
        silu_f = sb("silu_f", [P, 2, GW])
        gelu_f = sb("gelu_f", [P, 4, GW])
        gate_f = sb("gate_f", [P, 3, GW])
        hi_wide = sb("hi_wide", [P, GW])
        ho_hi = sb("ho_hi", [P, BG, M, GW], F16)
        ho_lo = sb("ho_lo", [P, BG, M, GW], F16)
        he_hi = sb("he_hi", [P, BG, M, GW], F16)
        he_lo = sb("he_lo", [P, BG, M, GW], F16)
        sink = sb("sink", [P, 2 * G * M + G])

        ps_row = ctx.enter_context(nc.psum_tensor("ps_row", [P, 2, 512], F32))
        ps_two = ctx.enter_context(nc.psum_tensor("ps_two", [P, 2, 512], F32))
        ps_up = ctx.enter_context(nc.psum_tensor("ps_up", [P, 4, 512], F32))

        x_in = [sem(f"x_in{g}") for g in range(G)]
        ident_in, cols_in, aw_in, s3_in, up_in, h1_in, h2_in, w3_in = (
            sem(n) for n in ("ident_in", "cols_in", "aw_in", "s3_in", "up_in", "h1_in", "h2_in", "w3_in"))
        ones_set = sem("ones_set")
        warm_set = sem("warm_set")
        pool_step = sem("pool_step")
        vec_step = sem("vec_step")
        z_abs_ready = sem("z_abs_ready")
        z_exp_ready = sem("z_exp_ready")
        rstd_ready = [None] + [sem(f"rstd_ready{n}") for n in (1, 2, 3)]
        centred = [None, sem("centred1"), None, sem("centred3")]
        base_ready = [sem(f"base_ready{n}") for n in range(4)]
        root_ready = sem("root_ready")
        root3_ready = sem("root3_ready")
        pow0_ready = sem("pow0_ready")
        gq_ready = sem("gq_ready")
        norm_ready = [None, None] + [sem(f"norm_ready{n}") for n in (2, 3)]
        n_rows_vec = sem("n_rows_vec")
        n_rows_pool = sem("n_rows_pool")
        nT_ready = sem("nT_ready")
        n_hi_ready = sem("n_hi_ready")
        n_lo_ready = sem("n_lo_ready")
        sim_ready = sem("sim_ready")
        relu_done = sem("relu_done")
        row_ready = sem("row_ready")
        count_ready = sem("count_ready")
        z_read = sem("z_read")
        softplus_log = sem("softplus_log")
        sp_ready = sem("sp_ready")
        sp_hi_ready = sem("sp_hi_ready")
        sp_lo_ready = sem("sp_lo_ready")
        pa_ready = sem("pa_ready")
        pb_ready = sem("pb_ready")
        y_done = sem("y_done")
        y2_done = sem("y2_done")
        aT_ready = sem("aT_ready")
        a_hi_ready = sem("a_hi_ready")
        a_lo_ready = sem("a_lo_ready")
        aw_hi_ready = sem("aw_hi_ready")
        aw_lo_ready = sem("aw_lo_ready")
        w_hi_ready = sem("w_hi_ready")
        w_his_ready = sem("w_his_ready")
        w_hi_pool = sem("w_hi_pool")
        w_his_pool = sem("w_his_pool")
        w_lo_ready = sem("w_lo_ready")
        lo_sq_ready = sem("lo_sq_ready")
        lo_any_ready = sem("lo_any_ready")
        lo_all_ready = sem("lo_all_ready")
        flag_ready = sem("flag_ready")
        colk_ready = sem("colk_ready")
        up_ready = sem("up_ready")
        silu_done = sem("silu_done")
        gate_done = sem("gate_done")
        up_hi_ready = sem("up_hi_ready")
        up_lo_vec = sem("up_lo_vec")
        up_lo_pool = sem("up_lo_pool")
        up_hi_wide = sem("up_hi_wide")
        hid_ready = sem("hid_ready")
        gelu_done = sem("gelu_done")
        hid_hi_ready = sem("hid_hi_ready")
        hid_lo_ready = sem("hid_lo_ready")
        down_ready = sem("down_ready")
        down_read = sem("down_read")
        out_ready = sem("out_ready")
        half_ready = sem("half_ready")
        out_stored = sem("out_stored")

        off_up = 0
        off_hid = [2 * HID, 2 * HID + M * HID]
        off_w3 = 2 * HID + 2 * M * HID
        blocks = [(off_up, off_hid[0], up_in), (off_hid[0], off_hid[1], h1_in),
                  (off_hid[1], off_w3, h2_in), (off_w3, off_w3 + M * D, w3_in)]
        parts = [(c, min(1024, c1 - c)) for c0, c1, _ in blocks for c in range(c0, c1, 1024)]

        def by_pool(m):
            return m == 1

        def low_made(n):
            g, m = divmod(n, M)
            if by_pool(m):
                return up_lo_pool, g + 1
            return up_lo_vec, g * (M - 1) + m + 1 - (m > 1)

        pool_high = [(c, loaded) for c0, c1, loaded in blocks[2:] for c in range(c0, c1, 512)]

        flag_parts = [1, len(parts)]

        def hid_index(layer, g, m):
            b, i = divmod(g, BG)
            return ((b * 2 + layer) * BG + i) * M + m

        HU = 2 * BG * M
        BATCH_TURNS = HU + BG
        DOWN_FIRST, DOWN_LAST = HU - 2, HU + 1

        def hid_turn(n):
            b, k = divmod(n, HU)
            return b * BATCH_TURNS + k + (k >= DOWN_FIRST)

        def down_turn(g):
            b, i = divmod(g, BG)
            return b * BATCH_TURNS + (DOWN_FIRST, DOWN_LAST)[i]

        def turn_read(turn):
            b, k = divmod(turn, BATCH_TURNS)
            if k in (DOWN_FIRST, DOWN_LAST):
                return down_read, b * BG + (1 if k == DOWN_FIRST else 2)
            return gelu_done, b * HU + k - (k > DOWN_FIRST) + 1

        def row_bank(g):
            return ps_up[:, g] if g < BG else ps_row[:, g % BG]

        def n_bank(g):
            return ps_row[:, g] if g < BG else ps_up[:, g - BG]

        def sim_bank(n):
            return ps_two[:, n % 4] if n % 4 < 2 else ps_up[:, n % 4]

        def up_bank(m, j):
            return ps_up[:, 2 * ((m + 1) % 2) + j]

        block = ctx.enter_context(nc.Block())

        @block.sync
        def _(sync):
            sync.dma_start(x[:, 0], x_dram[0]).then_inc(x_in[0], 16)
            sync.dma_start(x[:, 1], x_dram[1]).then_inc(x_in[1], 16)
            sync.dma_start(ident[:], identity).then_inc(ident_in, 16)
            sync.dma_start(aw[:].rearrange("p (k n) -> p k n", k=2), attn_w).then_inc(aw_in, 16)
            sync.dma_start(wf[:, 0:off_hid[0]], up_w).then_inc(up_in, 16)
            sync.dma_start(x[:, 2], x_dram[2]).then_inc(x_in[2], 16)
            sync.dma_start(x[:, 3], x_dram[3]).then_inc(x_in[3], 16)
            sync.dma_start(col[:], cols).then_inc(cols_in, 16)
            for off, w, s in ((off_hid[0], h1_w, h1_in), (off_hid[1], h2_w, h2_in)):
                sync.dma_start(wf[:, off:off + M * HID].rearrange("p (k n) -> p k n", k=M),
                               w.rearrange("(k p) n -> p k n", p=P)).then_inc(s, 16)
            sync.dma_start(wf[:, off_w3:off_w3 + M * D].rearrange("p (k n) -> p k n", k=M),
                           w3_w.rearrange("(k p) n -> p k n", p=P)).then_inc(w3_in, 16)
            sync.dma_start(s3b[:], s3_row.partition_broadcast(P)).then_inc(s3_in, 16)
            for g in range(BG):
                sync.wait_ge(out_ready, g + 1)
                sync.dma_start(out_dram[g], x1[:, g]).then_inc(out_stored, 16)
            for g in range(BG, G):
                for half in range(2):
                    sync.wait_ge(half_ready, 2 * (g - BG) + half + 1)
                    t = slice(half * GT // 2, (half + 1) * GT // 2)
                    sync.dma_start(out_dram[g][:, t], x1[:, g, t]).then_inc(out_stored, 16)
            sync.wait_ge(out_stored, 16 * (BG + 2 * (G - BG)))

        @block.gpsimd
        def _(pool):
            steps = [0]

            def step(ins):
                steps[0] += 1
                ins.then_inc(pool_step, 1)
                return steps[0]

            def row_length(g):
                pool.wait_ge(pow0_ready, g + 1)
                s = step(nc.gpsimd.tensor_tensor(gq[:, g], pow0[:, g, 0:GT], pow0[:, g, GT:2 * GT], ALU.mult))
                pool.wait_ge(pool_step, s)
                nc.gpsimd.tensor_tensor(gq[:, g], gq[:, g], base0[:, g, 0:GT], ALU.mult).then_inc(gq_ready, 1)

            def rstd_pow(n, g):
                pool.wait_ge(base_ready[n], g + 1)
                nc.gpsimd.tensor_tensor(rstd[:, n - 1, g], base[:, n - 1, g], neg_half[:, 0:GT],
                                        ALU.pow).then_inc(rstd_ready[n], 1)

            def normalise(n, g, src, dst, r, ts, done):
                s = step(nc.gpsimd.tensor_scalar(neg_mean[:, n, g], mv[:, n, g, :, 0], -1.0, 0.0,
                                                 ALU.mult, ALU.add))
                pool.wait_ge(pool_step, s)
                for t in ts:
                    ins = nc.gpsimd.tensor_scalar(dst[:, t], src[:, t], neg_mean[:, n, g, t:t + 1], r[:, t:t + 1],
                                                  ALU.add, ALU.mult)
                ins.then_inc(done, 1)

            def inverse_root(g):
                pool.wait_ge(base_ready[0], g + 1)
                nc.gpsimd.tensor_tensor(pow0[:, g], base0[:, g], neg_half[:], ALU.pow).then_inc(pow0_ready, 1)

            def n_rows(g, ts=range(GT)):
                pool.wait_ge(pow0_ready, g + 1)
                normalise(0, g, x[:, g], nrm[:, g], pow0[:, g, 0:GT], ts, n_rows_pool)

            def norm2(g):
                pool.wait_ge(rstd_ready[2], g + 1)
                normalise(2, g, x1[:, g], nrm[:, g], rstd[:, 1, g], range(GT), norm_ready[2])

            def norm3(g):
                pool.wait_ge(rstd_ready[3], g + 1)
                normalise(3, g, y[:, g % 2], y2[:, g % 2], rstd[:, 2, g], range(GT), norm_ready[3])

            def result(g):
                pool.wait_ge(norm_ready[3], g + 1)
                nc.gpsimd.tensor_tensor(x1[:, g], x1[:, g], y2[:, g % 2], ALU.add).then_inc(out_ready, 1)

            def weights_high(i):
                c, loaded = pool_high[i]
                w = slice(c, c + 512)
                pool.wait_ge(loaded, 16)
                nc.gpsimd.tensor_scalar(w_hi[:, w], wf[:, w], W_SCALE, 0.0, ALU.mult, ALU.add).then_inc(w_hi_pool, 1)
                pool.wait_ge(w_hi_pool, i + 1)
                nc.gpsimd.tensor_scalar(w_his[:, w], w_hi[:, w], 1.0 / LO_SCALE, 0.0, ALU.mult,
                                        ALU.add).then_inc(w_his_pool, 1)

            def softplus_hi(g):
                pool.wait_ge(sp_ready, g + 1)
                nc.gpsimd.tensor_scalar(sp_hi[:, g % 2], sp[:, g % 2], 1.0, 0.0,
                                        ALU.mult, ALU.add).then_inc(sp_hi_ready, 1)

            def up_hi(g, ms=range(M)):
                for m in ms:
                    n = M * g + m
                    pool.wait_ge(gate_done, n + 1)
                    nc.gpsimd.tensor_scalar(ho_hi[:, g % BG, m], gate_f[:, n % 3], 1.0 / LO_SCALE, 0.0,
                                            ALU.mult, ALU.add).then_inc(up_hi_ready, 1)
                    if by_pool(m):
                        pool.wait_ge(up_hi_ready, n + 1)
                        if g:
                            pool.wait_ge(up_lo_pool, g)
                        nc.gpsimd.tensor_scalar(hi_wide[:], ho_hi[:, g % BG, m], LO_SCALE, 0.0,
                                                ALU.mult, ALU.add).then_inc(up_hi_wide, 1)
                        pool.wait_ge(up_hi_wide, g + 1)
                        nc.gpsimd.tensor_tensor(ho_lo[:, g % BG, m], gate_f[:, n % 3], hi_wide[:],
                                                ALU.subtract).then_inc(up_lo_pool, 1)

            nc.gpsimd.memset(warm[:], 0.0).then_inc(warm_set, 1)
            nc.gpsimd.memset(ones[:], 1.0).then_inc(ones_set, 1)
            pool.wait_ge(pool_step, step(nc.gpsimd.memset(neg_half[:], -0.5)))
            row_length(0)
            row_length(1)
            n_rows(1, range(0, GT // 2))
            inverse_root(2)
            n_rows(2)
            row_length(2)
            weights_high(0)
            weights_high(1)
            inverse_root(3)
            n_rows(3)
            weights_high(2)
            softplus_hi(0)
            row_length(3)
            weights_high(3)
            rstd_pow(1, 0)
            softplus_hi(1)
            weights_high(4)
            rstd_pow(2, 0)
            rstd_pow(1, 1)
            rstd_pow(2, 1)
            softplus_hi(2)
            softplus_hi(3)
            up_hi(0)
            up_hi(1)
            rstd_pow(1, 2)
            rstd_pow(2, 2)
            norm2(2)
            rstd_pow(1, 3)
            rstd_pow(2, 3)
            norm2(3)
            up_hi(2)
            up_hi(3, range(0, 2))
            rstd_pow(3, 0)
            up_hi(3, range(2, 4))
            rstd_pow(3, 1)
            norm3(0)
            norm3(1)
            result(0)
            rstd_pow(3, 2)
            result(1)

        @block.scalar
        def _(act):
            def root(g):
                act.wait_ge(base_ready[0], g + 1)
                nc.scalar.activation(root0[:, g], base0[:, g], ACT.Sqrt).then_inc(root_ready, 1)

            def last_root():
                act.wait_ge(base_ready[3], G)
                nc.scalar.activation(root3[:], base[:, 2, G - 1], ACT.Sqrt).then_inc(root3_ready, 1)

            def squares(i):
                c, w = parts[i]
                act.wait_ge(w_lo_ready, i + 1)
                if i >= 2:
                    act.wait_ge(lo_sq_ready, i - 1)
                nc.scalar.activation(lo_sink[:, i % 2, 0:w], w_lo[:, c:c + w], ACT.Square,
                                     accum_out=lo_sq[:, i:i + 1]).then_inc(lo_sq_ready, 1)

            def n_high(g):
                act.wait_ge(nT_ready, g + 1)
                nc.scalar.copy(n_hi[:, g * GW:(g + 1) * GW], n_bank(g)).then_inc(n_hi_ready, 1)

            def relu_sums(b, us):
                for u in us:
                    i, h = units[u]
                    n = b * NU + u
                    act.wait_ge(sim_ready, n + 1)
                    if n >= 2:
                        act.wait_ge(relu_done, n - 1)
                    nc.scalar.activation(relu_sink[:, n % 2], sim_bank(n), ACT.Relu,
                                         accum_out=rows[:, b, h, i:i + 1]).then_inc(relu_done, 1)

            def softplus_z(g):
                act.wait_ge(count_ready, g + 1)
                act.wait_ge(colk_ready, 1)
                if g >= 2:
                    act.wait_ge(sp_ready, g - 1)
                w1c, b1c = colk[:, 4 * M:4 * M + 1], col[:, 4 * M + 1:4 * M + 2]
                nc.scalar.activation(z_abs[:, g % 2], ps_row[:, g % 2], ACT.Abs, bias=b1c,
                                     scale=w1c).then_inc(z_abs_ready, 1)
                nc.scalar.activation(z_pos[:, g % 2], ps_row[:, g % 2], ACT.Relu, bias=b1c,
                                     scale=w1c).then_inc(z_read, 1)

            def softplus_ln(g):
                z = z_abs[:, g % 2]
                act.wait_ge(z_abs_ready, g + 1)
                nc.scalar.activation(z, z, ACT.Exp, scale=-1.0).then_inc(z_exp_ready, 1)
                act.wait_ge(z_exp_ready, g + 1)
                nc.scalar.activation(z, z, ACT.Ln, bias=1.0).then_inc(softplus_log, 1)

            def a_high(g):
                act.wait_ge(aT_ready, g + 1)
                nc.scalar.copy(a_hi[:, g], row_bank(g)).then_inc(a_hi_ready, 1)

            def silu(g, ms):
                for m in ms:
                    n = M * g + m
                    act.wait_ge(up_ready, 2 * n + 1)
                    if n >= 2:
                        act.wait_ge(gate_done, n - 1)
                    nc.scalar.activation(silu_f[:, n % 2], up_bank(m, 0), ACT.Silu,
                                         scale=colk[:, m:m + 1]).then_inc(silu_done, 1)

            def gelu(layer, g, ms=range(M)):
                dst = (he_hi, ho_hi)[layer]
                scale = colk[:, (2 + layer) * M:(3 + layer) * M]
                for m in ms:
                    n = hid_index(layer, g, m)
                    src = ps_two[:, hid_turn(n) % 2]
                    act.wait_ge(hid_ready, n + 1)
                    nc.scalar.activation(dst[:, g % BG, m], src, ACT.Gelu,
                                         scale=scale[:, m:m + 1]).then_inc(hid_hi_ready, 1)
                    if n >= 4:
                        act.wait_ge(hid_lo_ready, n - 3)
                    nc.scalar.activation(gelu_f[:, n % 4], src, ACT.Gelu,
                                         scale=scale[:, m:m + 1]).then_inc(gelu_done, 1)

            act.wait_ge(aw_in, 16)
            nc.scalar.activation(aw_hi[:], aw[:], ACT.Copy, scale=W_SCALE).then_inc(aw_hi_ready, 1)
            root(0)
            root(1)
            n_high(0)
            n_high(1)
            relu_sums(0, [0])
            nc.scalar.preload_act_table_set("natural_log_exp_and_others")
            relu_sums(0, range(1, 6))
            n_high(2)
            relu_sums(0, range(6, 9))
            softplus_z(0)
            relu_sums(0, [9])
            softplus_ln(0)
            relu_sums(0, range(10, 12))
            n_high(3)
            relu_sums(0, range(12, 16))
            relu_sums(1, [0])
            softplus_z(1)
            softplus_ln(1)
            relu_sums(1, range(1, 5))
            squares(0)
            relu_sums(1, range(5, 8))
            squares(1)
            relu_sums(1, [8])
            softplus_z(2)
            relu_sums(1, [9])
            softplus_ln(2)
            relu_sums(1, range(10, 16))
            a_high(0)
            squares(2)
            softplus_z(3)
            a_high(1)
            softplus_ln(3)
            nc.scalar.preload_act_table_set("silu_and_others")
            silu(0, range(0, 2))
            squares(3)
            silu(0, range(2, 4))
            squares(4)
            squares(5)
            silu(1, range(0, 4))
            gelu(0, 0)
            gelu(0, 1)
            gelu(1, 0)
            gelu(1, 1, range(0, 3))
            a_high(2)
            gelu(1, 1, [3])
            silu(2, range(0, 4))
            a_high(3)
            silu(3, range(0, 4))
            gelu(0, 2)
            gelu(0, 3)
            gelu(1, 2)
            gelu(1, 3)
            last_root()
            nc.scalar.preload_act_table_set("sqrt_and_others")

        @block.tensor
        def _(pe):
            def n_transpose(g):
                if g == 0:
                    pe.wait_ge(ident_in, 16)
                if g < 2:
                    pe.wait_ge(n_rows_vec, g + 1)
                if g:
                    pe.wait_ge(n_rows_pool, g)
                for t in range(GT):
                    mm = nc.tensor.transpose(n_bank(g)[:, t * P:(t + 1) * P], nrm[:, g, t], ident[:])
                mm.then_inc(nT_ready, 1)

            def similarity(b, us):
                for u in us:
                    i, h = units[u]
                    n = b * NU + u
                    if u in (0, GT):
                        pe.wait_ge(n_lo_ready, BG * b + h + 1)
                    if n >= 4:
                        pe.wait_ge(relu_done, n - 3)
                    r = slice(b * BW + i * P, b * BW + (i + 1) * P)
                    c = slice(b * BW + h * GW, b * BW + (h + 1) * GW)
                    dst = sim_bank(n)
                    nc.tensor.matmul(dst, n_hi[:, r], n_hi[:, c], start=True, stop=False)
                    nc.tensor.matmul(dst, n_hi[:, r], n_lo[:, c], start=False, stop=False)
                    nc.tensor.matmul(dst, n_lo[:, r], n_hi[:, c], start=False,
                                     stop=True).then_inc(sim_ready, 1)

            def counter(g):
                b, i = divmod(g, BG)
                if b:
                    pe.wait_ge(z_read, g - 1)
                pe.wait_ge(row_ready, g + 1)
                for t in range(GT):
                    j = i * GT + t
                    mm = nc.tensor.matmul(ps_row[:, i, t * P:(t + 1) * P],
                                          row[:, b, j:j + 1].to_broadcast([P, P]), ident[:], start=True, stop=True)
                mm.then_inc(count_ready, 1)

            def row_product(dst, hi, lo, w):
                for t in range(GT):
                    o = dst[:, t * P:(t + 1) * P]
                    c = slice(t * P, (t + 1) * P)
                    nc.tensor.matmul(o, hi[:, c], aw_hi[:, w], start=True, stop=False)
                    nc.tensor.matmul(o, hi[:, c], aw_lo[:, w], start=False, stop=False)
                    mm = nc.tensor.matmul(o, lo[:, c], aw_hi[:, w], start=False, stop=True)
                return mm

            def attn_data(g):
                if g == 0:
                    pe.wait_ge(aw_lo_ready, 1)
                pe.wait_ge(n_lo_ready, g + 1)
                if g < BG:
                    pe.wait_ge(n_lo_ready, g + 3)
                else:
                    pe.wait_ge(z_read, g + 1)
                c = slice(g * GW, (g + 1) * GW)
                row_product(row_bank(g), n_hi[:, c], n_lo[:, c], slice(0, D)).then_inc(pa_ready, 1)

            def attn_counter(g):
                pe.wait_ge(sp_hi_ready, g + 1)
                pe.wait_ge(sp_lo_ready, g + 1)
                pe.wait_ge(y_done, g + 1)
                row_product(row_bank(g), sp_hi[:, g % 2], sp_lo[:, g % 2],
                            slice(D, 2 * D)).then_inc(pb_ready, 1)

            def a_transpose(g):
                pe.wait_ge(norm_ready[2], g + 1)
                pe.wait_ge(y2_done, g + 1)
                for t in range(GT):
                    mm = nc.tensor.transpose(row_bank(g)[:, t * P:(t + 1) * P], nrm[:, g, t], ident[:])
                mm.then_inc(aT_ready, 1)

            def product(dst, w_col, hi, lo, first, last, general):
                w = slice(w_col, w_col + P)
                nc.tensor.matmul(dst, w_hi[:, w], hi, start=first, stop=False)
                if general:
                    nc.tensor.matmul(dst, w_lo[:, w], hi, start=False, stop=False)
                return nc.tensor.matmul(dst, w_his[:, w], lo, start=False, stop=last)

            def up(g, general, ms=range(M)):
                pe.wait_ge(a_hi_ready, g + 1)
                pe.wait_ge(a_lo_ready, g + 1)
                for m in ms:
                    n = M * g + m
                    if n == 0:
                        pe.wait_ge(relu_done, B * NU)
                    elif n == 1:
                        pe.wait_ge(a_lo_ready, BG)
                    else:
                        pe.wait_ge(gate_done, n - 1)
                    for j in range(2):
                        product(up_bank(m, j), off_up + j * HID + m * P, a_hi[:, g], a_lo[:, g],
                                True, True, general).then_inc(up_ready, 1)

            def hidden(layer, g, general, ms=range(M)):
                src_hi, src_lo = ((ho_hi, ho_lo), (he_hi, he_lo))[layer]
                for m in ms:
                    n = hid_index(layer, g, m)
                    turn = hid_turn(n)
                    if turn >= 2:
                        pe.wait_ge(*turn_read(turn - 2))
                    else:
                        pe.wait_ge(relu_done, B * NU)
                    if turn == 0:
                        pe.wait_ge(flag_ready, 2)
                    for k in range(M):
                        if m == 0 and layer == 0:
                            pe.wait_ge(up_hi_ready, M * g + k + 1)
                            pe.wait_ge(*low_made(M * g + k))
                        elif m == 0:
                            pe.wait_ge(hid_hi_ready, hid_index(0, g, k) + 1)
                            pe.wait_ge(hid_lo_ready, hid_index(0, g, k) + 1)
                        mm = product(ps_two[:, turn % 2], off_hid[layer] + k * HID + m * P, src_hi[:, g % BG, k],
                                     src_lo[:, g % BG, k], k == 0, k == M - 1, general)
                    mm.then_inc(hid_ready, 1)

            def down(g, general):
                turn = down_turn(g)
                pe.wait_ge(*turn_read(turn - 2))
                for k in range(M):
                    pe.wait_ge(hid_hi_ready, hid_index(1, g, k) + 1)
                    pe.wait_ge(hid_lo_ready, hid_index(1, g, k) + 1)
                    w = slice(off_w3 + k * D, off_w3 + (k + 1) * D)
                    for t in range(GT):
                        o = ps_two[:, turn % 2, t * P:(t + 1) * P]
                        c = slice(t * P, (t + 1) * P)
                        hi, lo = ho_hi[:, g % BG, k, c], ho_lo[:, g % BG, k, c]
                        nc.tensor.matmul(o, hi, w_hi[:, w], start=(k == 0 and t == 0), stop=False)
                        if general:
                            nc.tensor.matmul(o, hi, w_lo[:, w], start=False, stop=False)
                        mm = nc.tensor.matmul(o, lo, w_his[:, w], start=False,
                                              stop=(k == M - 1 and t == GT - 1))
                mm.then_inc(down_ready, 1)

            def flag_total(j):
                pe.wait_ge(lo_any_ready, j + 1)
                if j == 0:
                    pe.wait_ge(ones_set, 1)
                    pe.wait_ge(relu_done, B * NU - 3)
                else:
                    pe.wait_ge(flag_ready, 1)
                nc.tensor.matmul(ps_two[0:1, 0, 0:2], lo_any[:, j:j + 1], ones[:, 0:2], start=True,
                                 stop=True).then_inc(lo_all_ready, 1)

            def flag_value(j):
                pe.wait_ge(flag_ready, j + 1)
                return pe.value_load(flag[0:1, j:j + 1].bitcast(I32), min_val=0, max_val=2**31 - 1)

            def gated_layer(general):
                up(0, general)
                attn_data(2)
                up(1, general, range(0, 2))
                flag_total(1)
                up(1, general, range(2, 4))


            def later_layers(general):
                attn_data(3)
                attn_counter(2)
                hidden(0, 0, general)
                hidden(0, 1, general)
                hidden(1, 0, general, [0])
                attn_counter(3)
                hidden(1, 0, general, range(1, 3))
                a_transpose(2)
                hidden(1, 0, general, [3])
                hidden(1, 1, general, range(0, 2))
                down(0, general)
                hidden(1, 1, general, range(2, 4))
                up(2, general, [0])
                a_transpose(3)
                up(2, general, range(1, 4))
                down(1, general)
                up(3, general)
                hidden(0, 2, general)
                hidden(0, 3, general)
                hidden(1, 2, general)
                hidden(1, 3, general, range(0, 2))
                down(2, general)
                hidden(1, 3, general, range(2, 4))
                down(3, general)


            pe.wait_ge(warm_set, 1)
            for _ in range(WARM_UP):
                nc.tensor.matmul(ps_up[:, 0], warm[:, 0:P], warm[:], start=True, stop=True)
            n_transpose(0)
            n_transpose(1)
            similarity(0, range(0, 7))
            n_transpose(2)
            similarity(0, range(7, 9))
            counter(0)
            attn_data(0)
            similarity(0, [9])
            n_transpose(3)
            similarity(0, range(10, 16))
            similarity(1, [0])
            attn_counter(0)
            attn_data(1)
            counter(1)
            similarity(1, range(1, 8))
            attn_counter(1)
            similarity(1, range(8, 11))
            counter(2)
            similarity(1, range(11, 15))
            a_transpose(0)
            similarity(1, [15])
            flag_total(0)
            counter(3)
            a_transpose(1)

            pe.wait_ge(w_his_ready, 2)
            pe.wait_ge(w_his_pool, len(pool_high))
            with pe.If(flag_value(0) != 0):
                gated_layer(True)
            with pe.Else():
                gated_layer(False)
            with pe.If(flag_value(1) != 0):
                later_layers(True)
            with pe.Else():
                later_layers(False)

        @block.vector
        def _(dve):
            steps = [0]

            def step(ins):
                steps[0] += 1
                ins.then_inc(vec_step, 1)
                return steps[0]

            def moments(n, g, src):
                for t in range(GT):
                    s = step(nc.vector.bn_stats(stats[:, n, g % 2, t], src[:, t]))
                for t in range(GT):
                    dve.wait_ge(vec_step, s - GT + 1 + t)
                    e = step(nc.vector.bn_aggr(mv[:, n, g, t], stats[:, n, g % 2, t]))
                dve.wait_ge(vec_step, e)

            def moments_plus(n, g, src, eps):
                moments(n, g, src)
                nc.vector.tensor_scalar(base[:, n - 1, g], mv[:, n, g, :, 1], eps, None,
                                        ALU.add).then_inc(base_ready[n], 1)

            def ln0(g):
                dve.wait_ge(x_in[g], 16)
                moments(0, g, x[:, g])
                var = mv[:, 0, g, :, 1]
                k = 1.0 / (N_SCALE * N_SCALE)
                step(nc.vector.tensor_scalar(small[:, g], var, EPS, MIN_SQ * k, ALU.add, ALU.mult))
                s = step(nc.vector.tensor_scalar(base0[:, g, GT:2 * GT], var, EPS, None, ALU.add))
                dve.wait_ge(vec_step, s)
                nc.vector.scalar_tensor_tensor(out=base0[:, g, 0:GT], in0=var, scalar=D * k, in1=small[:, g],
                                               op0=ALU.mult, op1=ALU.max).then_inc(base_ready[0], 1)

            def inverse_root(g):
                dve.wait_ge(root_ready, g + 1)
                nc.vector.reciprocal(pow0[:, g], root0[:, g]).then_inc(pow0_ready, 1)

            def n_rows(g, ts):
                dve.wait_ge(pow0_ready, g + 1)
                for t in ts:
                    ins = nc.vector.tensor_scalar(nrm[:, g, t], x[:, g, t], mv[:, 0, g, t, 0:1],
                                                  pow0[:, g, t:t + 1], ALU.subtract, ALU.mult)
                ins.then_inc(n_rows_vec, 1)

            def n_low(g):
                dve.wait_ge(n_hi_ready, g + 1)
                c = slice(g * GW, (g + 1) * GW)
                nc.vector.tensor_tensor(n_lo[:, c], n_bank(g), n_hi[:, c], ALU.subtract).then_inc(n_lo_ready, 1)

            def row_sums(g):
                b, i = divmod(g, BG)
                dve.wait_ge(relu_done, b * NU + (i + 1) * UH)
                c = slice(i * GT, (i + 1) * GT)
                nc.vector.tensor_tensor(row[:, b, c], rows[:, b, 0, c], rows[:, b, 1, c],
                                        ALU.add).then_inc(row_ready, 1)

            def softplus_sum(g):
                dve.wait_ge(softplus_log, g + 1)
                dve.wait_ge(z_read, g + 1)
                if g >= 2:
                    dve.wait_ge(sp_lo_ready, g - 1)
                nc.vector.tensor_tensor(sp[:, g % 2], z_abs[:, g % 2], z_pos[:, g % 2], ALU.add).then_inc(sp_ready, 1)

            def softplus_low(g):
                dve.wait_ge(sp_hi_ready, g + 1)
                nc.vector.tensor_tensor(sp_lo[:, g % 2], sp[:, g % 2], sp_hi[:, g % 2],
                                        ALU.subtract).then_inc(sp_lo_ready, 1)

            def scale_data(g):
                dve.wait_ge(pa_ready, g + 1)
                dve.wait_ge(gq_ready, g + 1)
                nc.vector.tensor_tensor(y[:, g % 2], row_bank(g).rearrange("p (t d) -> p t d", t=GT),
                                        gq[:, g].unsqueeze(2).to_broadcast([P, GT, D]), ALU.mult).then_inc(y_done, 1)

            def attn_out(g):
                dve.wait_ge(pb_ready, g + 1)
                dve.wait_ge(y_done, g + 1)
                nc.vector.tensor_tensor(y2[:, g % 2], row_bank(g).rearrange("p (t d) -> p t d", t=GT),
                                        y[:, g % 2], ALU.add).then_inc(y2_done, 1)

            def attn_moments(g):
                dve.wait_ge(y2_done, g + 1)
                moments_plus(1, g, y2[:, g % 2], EPS * W_SCALE * W_SCALE)
                centre(1, g, y[:, g % 2], y2[:, g % 2])

            def centre(n, g, dst, src):
                nc.vector.tensor_tensor(dst, src, mv[:, n, g, :, 0].unsqueeze(2).to_broadcast([P, GT, D]),
                                        ALU.subtract).then_inc(centred[n], 1)

            def residual(g):
                dve.wait_ge(rstd_ready[1], g + 1)
                dve.wait_ge(centred[1], g + 1)
                for t in range(GT):
                    s = step(nc.vector.scalar_tensor_tensor(out=x1[:, g, t], in0=y[:, g % 2, t],
                                                            scalar=rstd[:, 0, g, t:t + 1], in1=x[:, g, t],
                                                            op0=ALU.mult, op1=ALU.add))
                dve.wait_ge(vec_step, s)
                moments_plus(2, g, x1[:, g], EPS)

            def norm2(g):
                dve.wait_ge(rstd_ready[2], g + 1)
                for t in range(GT):
                    ins = nc.vector.tensor_scalar(nrm[:, g, t], x1[:, g, t], mv[:, 2, g, t, 0:1],
                                                  rstd[:, 1, g, t:t + 1], ALU.subtract, ALU.mult)
                ins.then_inc(norm_ready[2], 1)

            def scaled_low(dst, src, hi, n):
                return nc.vector.tensor_tensor_reduce(dst, src, hi, LO_SCALE, 0.0, ALU.subtract, ALU.max,
                                                      sink[:, n:n + 1])

            def a_low(g):
                dve.wait_ge(a_hi_ready, g + 1)
                scaled_low(a_lo[:, g], row_bank(g), a_hi[:, g], 2 * G * M + g).then_inc(a_lo_ready, 1)

            def gate(g, m):
                n = M * g + m
                dve.wait_ge(up_ready, 2 * n + 2)
                dve.wait_ge(silu_done, n + 1)
                if n >= 3:
                    dve.wait_ge(up_hi_ready, n - 2)
                    dve.wait_ge(*low_made(n - 3))
                nc.vector.scalar_tensor_tensor(out=gate_f[:, n % 3], in0=up_bank(m, 1),
                                               scalar=colk[:, M + m:M + m + 1], in1=silu_f[:, n % 2],
                                               op0=ALU.mult, op1=ALU.mult).then_inc(gate_done, 1)

            def gate_low(g, m):
                n = M * g + m
                dve.wait_ge(up_hi_ready, n + 1)
                nc.vector.scalar_tensor_tensor(out=ho_lo[:, g % BG, m], in0=ho_hi[:, g % BG, m],
                                               scalar=-LO_SCALE, in1=gate_f[:, n % 3], op0=ALU.mult,
                                               op1=ALU.add).then_inc(up_lo_vec, 1)

            def hid_low(layer, g, ms=range(M)):
                src, dst = ((he_hi, he_lo), (ho_hi, ho_lo))[layer]
                for m in ms:
                    n = hid_index(layer, g, m)
                    dve.wait_ge(gelu_done, n + 1)
                    scaled_low(dst[:, g % BG, m], gelu_f[:, n % 4], src[:, g % BG, m], n).then_inc(hid_lo_ready, 1)

            def ffn_out(g):
                dve.wait_ge(down_ready, g + 1)
                if g == 0:
                    dve.wait_ge(s3_in, 16)
                if g >= BG:
                    dve.wait_ge(norm_ready[3], g - 1)
                nc.vector.tensor_tensor(y[:, g % 2], ps_two[:, down_turn(g) % 2].rearrange("p (t d) -> p t d", t=GT),
                                        s3b[:].unsqueeze(1).to_broadcast([P, GT, D]),
                                        ALU.mult).then_inc(down_read, 1)

            def ffn_moments(g):
                dve.wait_ge(down_read, g + 1)
                moments_plus(3, g, y[:, g % 2], EPS * W_SCALE * W_SCALE)
                if g >= BG:
                    dve.wait_ge(out_ready, g - 1)
                    centre(3, g, y2[:, g % 2], y[:, g % 2])

            def result(g):
                if g == G - 1:
                    dve.wait_ge(root3_ready, 1)
                    nc.vector.reciprocal(rstd[:, 2, g], root3[:]).then_inc(rstd_ready[3], 1)
                dve.wait_ge(rstd_ready[3], g + 1)
                dve.wait_ge(centred[3], g - 1)
                for t in range(GT):
                    ins = nc.vector.scalar_tensor_tensor(out=x1[:, g, t], in0=y2[:, g % 2, t],
                                                         scalar=rstd[:, 2, g, t:t + 1], in1=x1[:, g, t],
                                                         op0=ALU.mult, op1=ALU.add)
                    if t % 2:
                        ins.then_inc(half_ready, 1)

            def weights_high(n):
                c0, c1, loaded = blocks[n]
                dve.wait_ge(loaded, 16)
                nc.vector.tensor_scalar(w_hi[:, c0:c1], wf[:, c0:c1], W_SCALE, None, ALU.mult).then_inc(w_hi_ready, 1)
                dve.wait_ge(w_hi_ready, n + 1)
                nc.vector.tensor_scalar(w_his[:, c0:c1], w_hi[:, c0:c1], 1.0 / LO_SCALE, None,
                                        ALU.mult).then_inc(w_his_ready, 1)

            def weights_low(i):
                c, w = parts[i]
                n = sum(c >= c1 for _, c1, _ in blocks)
                if n < 2:
                    dve.wait_ge(w_hi_ready, n + 1)
                else:
                    dve.wait_ge(w_hi_pool, sum(k < c + w for k, _ in pool_high))
                nc.vector.scalar_tensor_tensor(out=w_lo[:, c:c + w], in0=wf[:, c:c + w], scalar=W_SCALE,
                                               in1=w_hi[:, c:c + w], op0=ALU.mult,
                                               op1=ALU.subtract).then_inc(w_lo_ready, 1)

            def flag_sum(j):
                dve.wait_ge(lo_sq_ready, flag_parts[j])
                nc.vector.tensor_reduce(lo_any[:, j:j + 1], lo_sq[:, 0:flag_parts[j]], AX.X,
                                        ALU.add).then_inc(lo_any_ready, 1)

            def flag_out(j):
                dve.wait_ge(lo_all_ready, j + 1)
                nc.vector.tensor_copy(flag[:, j:j + 1], ps_two[0:1, 0, 0:1]).then_inc(flag_ready, 1)

            ln0(0)
            ln0(1)
            inverse_root(0)
            inverse_root(1)
            n_rows(0, range(GT))
            n_rows(1, range(GT // 2, GT))
            ln0(2)
            n_low(0)
            weights_high(0)
            n_low(1)
            ln0(3)
            weights_high(1)
            dve.wait_ge(aw_hi_ready, 1)
            nc.vector.scalar_tensor_tensor(out=aw_lo[:], in0=aw[:], scalar=W_SCALE, in1=aw_hi[:], op0=ALU.mult,
                                           op1=ALU.subtract).then_inc(aw_lo_ready, 1)
            weights_low(0)
            n_low(2)
            dve.wait_ge(cols_in, 16)
            step(nc.vector.tensor_scalar(colk[:, 0:M], col[:, 0:M], 1.0 / W_SCALE, None, ALU.mult))
            step(nc.vector.tensor_scalar(colk[:, M:2 * M], col[:, M:2 * M], LO_SCALE / W_SCALE, None, ALU.mult))
            step(nc.vector.tensor_scalar(colk[:, 2 * M:4 * M], col[:, 2 * M:4 * M], 1.0 / W_SCALE, None, ALU.mult))
            nc.vector.tensor_scalar(colk[:, 4 * M:4 * M + 1], col[:, 4 * M:4 * M + 1],
                                    1.0 / (N_SCALE * N_SCALE), None, ALU.mult).then_inc(colk_ready, 1)
            row_sums(0)
            weights_low(1)
            weights_low(2)
            scale_data(0)
            softplus_sum(0)
            n_low(3)
            softplus_low(0)
            row_sums(1)
            attn_out(0)
            attn_moments(0)
            scale_data(1)
            softplus_sum(1)
            softplus_low(1)
            residual(0)
            attn_out(1)
            row_sums(2)
            attn_moments(1)
            weights_low(3)
            norm2(0)
            residual(1)
            flag_sum(0)
            row_sums(3)
            norm2(1)
            softplus_sum(2)
            weights_low(4)
            flag_out(0)
            softplus_low(2)
            a_low(0)
            a_low(1)
            softplus_sum(3)
            gate(0, 0)
            gate(0, 1)
            weights_low(5)
            gate_low(0, 0)
            gate(0, 2)
            gate(0, 3)
            scale_data(2)
            flag_sum(1)
            gate_low(0, 2)
            gate(1, 0)
            gate(1, 1)
            flag_out(1)
            softplus_low(3)
            gate_low(0, 3)
            gate(1, 2)
            gate_low(1, 0)
            gate_low(1, 2)
            gate(1, 3)
            hid_low(0, 0, range(0, 2))
            gate_low(1, 3)
            hid_low(0, 0, [2])
            attn_out(2)
            hid_low(0, 0, [3])
            attn_moments(2)
            scale_data(3)
            hid_low(0, 1, [0])
            residual(2)
            hid_low(0, 1, [1])
            attn_out(3)
            hid_low(0, 1, [2])
            attn_moments(3)
            hid_low(0, 1, [3])
            hid_low(1, 0, range(0, 2))
            residual(3)
            hid_low(1, 0, range(2, 4))
            hid_low(1, 1, [0])
            ffn_out(0)
            ffn_moments(0)
            a_low(2)
            hid_low(1, 1, range(1, 4))
            gate(2, 0)
            gate(2, 1)
            gate(2, 2)
            gate_low(2, 0)
            a_low(3)
            gate(2, 3)
            gate_low(2, 2)
            gate(3, 0)
            gate(3, 1)
            gate_low(2, 3)
            gate_low(3, 0)
            gate(3, 2)
            ffn_out(1)
            gate(3, 3)
            hid_low(0, 2, [0])
            gate_low(3, 2)
            gate_low(3, 3)
            hid_low(0, 2, [1])
            ffn_moments(1)
            hid_low(0, 2, range(2, 4))
            hid_low(0, 3)
            hid_low(1, 2)
            hid_low(1, 3, range(0, 2))
            ffn_out(2)
            ffn_moments(2)
            hid_low(1, 3, [2])
            result(2)
            hid_low(1, 3, [3])
            ffn_out(3)
            ffn_moments(3)
            result(3)

def kernel(**inputs):
    import numpy as np
    import concourse.bacc as bacc
    from concourse.bass_utils import run_bass_kernel_spmd

    f = {n.removeprefix("L0_"): np.asarray(a) for n, a in inputs.items()}
    tokens = f["attn_data"].reshape(-1, f["attn_data"].shape[-1])
    columns = [f[n].reshape(-1, P).T for n in ("ffn_w1_s", "ffn_w2_s", "ffn_h1_s", "ffn_h2_s", "attn_W1", "attn_b1")]
    arrays = {
        "data": tokens,
        "identity": np.eye(P, dtype=np.float32),
        "cols": np.concatenate(columns, axis=1),
        "attn_w": f["attn_W2"].reshape(2, P, P).transpose(1, 0, 2),
        "up_w": np.concatenate([f["ffn_w1_w"].T, f["ffn_w2_w"].T], axis=1),
        "h1_w": f["ffn_h1_w"].T,
        "h2_w": f["ffn_h2_w"].T,
        "w3_w": f["ffn_w3_w"].T,
        "s3_row": f["ffn_w3_s"],
    }
    arrays = {n: np.ascontiguousarray(a) for n, a in arrays.items()}
    nc = bacc.Bacc("TRN2", target_bir_lowering=False, num_devices=1)
    dram = [nc.dram_tensor(n, a.shape, mybir.dt.from_np(a.dtype), kind="ExternalInput").ap()
            for n, a in arrays.items()]
    out = nc.dram_tensor("out", tokens.shape, F32, kind="ExternalOutput").ap()
    build(nc, *dram, out)
    r = run_bass_kernel_spmd(nc, [arrays], core_ids=[0])
    return r.results[0]["out"].reshape(f["attn_data"].shape)
```
